# Optimizing a Trainium2 kernel written in Bass

```python
import numpy as np
import jax
import jax.numpy as jnp

def _softmax(x, axis=-1):
    return jax.nn.softmax(x, axis=axis)

def _gelu(x):
    return jax.nn.gelu(x, approximate=True)

def _silu(x):
    return jax.nn.silu(x)

def _sigmoid(x):
    return jax.nn.sigmoid(x)

def _layernorm(x, axis=-1, eps=1e-05):
    m = jnp.mean(x, axis=axis, keepdims=True)
    v = jnp.var(x, axis=axis, keepdims=True)
    return (x - m) / jnp.sqrt(v + eps)

def _scatter_add(tgt, idx, src, axis=0):
    return tgt.at[idx].add(src)

def _segment_sum(src, seg, n):
    return jax.ops.segment_sum(src, seg, n)
kernel_name = 'mk_adj_resnorm_d4_adj_r2_a52e85'

def setup_inputs(seed: int=0):
    np.random.seed(seed)
    _w = jnp.asarray

    def _rec_inputs():
        import jax
        import jax.numpy as jnp
        _gk = jax.random.key(seed)
        x = -0.000929 + 1 * jax.random.normal(jax.random.fold_in(_gk, 1), (8, 1024, 64), jnp.float32)
        _a = jax.random.bernoulli(jax.random.fold_in(_gk, 2), 0.00390625, (1024, 1024))
        _a = jnp.logical_or(_a, jnp.swapaxes(_a, -1, -2))
        _a = jnp.logical_or(_a, jnp.eye(1024, dtype=bool))
        _af = _a.astype(jnp.float32)
        adj = _af
        return (x, adj)
    x, adj = _rec_inputs()

    def _L0_gnn_setup():
        import jax, jax.numpy as jnp
        import numpy as np
        NEG_INF = -1e+16

        def gat_layer(x, graph, W, b):
            h = x @ W
            s = jnp.einsum('bnd,bmd->bnm', h, h) * graph
            s = jnp.where(s == 0.0, NEG_INF, s)
            a = jax.nn.softmax(s, axis=2)
            return jnp.einsum('bnm,bmd->bnd', a, h) + b
        key = jax.random.key(seed)
        k1, k2, k3, k4, k5, k6 = jax.random.split(key, 6)
        B, N, C_IN, HID, HEADS, C_OUT = (16, 512, 64, 128, 8, 64)
        flow_x = jax.random.normal(k1, (B, N, C_IN), dtype=jnp.float32)
        graph = jax.random.randint(k2, (N, N), 0, 2).astype(jnp.float32)
        Wh = jax.random.normal(k3, (HEADS, C_IN, HID), dtype=jnp.float32)
        bh = jax.random.normal(k4, (HEADS, HID), dtype=jnp.float32)
        W_out = jax.random.normal(k5, (HID * HEADS, C_OUT), dtype=jnp.float32)
        b_out = jax.random.normal(k6, (C_OUT,), dtype=jnp.float32)
        return {'flow_x': flow_x, 'graph': graph, 'Wh': Wh, 'bh': bh, 'W_out': W_out, 'b_out': b_out}
    _L0_gnn_all = _L0_gnn_setup()
    _L0_gnn_in = {k: v for k, v in _L0_gnn_all.items() if k in ('Wh', 'bh', 'W_out', 'b_out')}
    del _L0_gnn_all

    def _L1_gnn_setup():
        import jax, jax.numpy as jnp
        import numpy as np
        key = jax.random.key(seed)
        ks = jax.random.split(key, 5)
        B, N, IN, OUT, K, D = (32, 1024, 64, 64, 3, 16)
        x = jax.random.normal(ks[0], (B, N, IN), dtype=jnp.float32)
        A = jax.random.uniform(ks[1], (N, N), dtype=jnp.float32)
        A = A / jnp.sum(A, axis=-1, keepdims=True)
        embedding = jax.random.normal(ks[2], (N, D), dtype=jnp.float32) * 0.3
        weight = jax.random.normal(ks[3], (D, K, IN, OUT), dtype=jnp.float32) * 0.1
        bias = jax.random.normal(ks[4], (D, OUT), dtype=jnp.float32) * 0.1
        return {'x': x, 'A': A, 'embedding': embedding, 'weight': weight, 'bias': bias}
    _L1_gnn_all = _L1_gnn_setup()
    _L1_gnn_in = {k: v for k, v in _L1_gnn_all.items() if k in ('embedding', 'weight', 'bias')}
    del _L1_gnn_all

    def _L2_gnn_setup():
        import jax, jax.numpy as jnp
        import numpy as np
        MAX_STEPS = 3
        key = jax.random.key(seed)
        ks = jax.random.split(key, 7)
        B, N, D = (1, 4096, 64)
        return {'causal_vars': jax.random.normal(ks[0], (B, N, D), dtype=jnp.float32), 'adj_matrix': jax.random.uniform(ks[1], (N, N), dtype=jnp.float32), 'intervention_value': jax.random.normal(ks[2], (B, D), dtype=jnp.float32), 'W1': jax.random.normal(ks[3], (D, 2 * D), dtype=jnp.float32) * (1.0 / np.sqrt(2 * D)), 'b1': jax.random.normal(ks[4], (D,), dtype=jnp.float32) * 0.01, 'W2': jax.random.normal(ks[5], (D, D), dtype=jnp.float32) * (1.0 / np.sqrt(D)), 'b2': jax.random.normal(ks[6], (D,), dtype=jnp.float32) * 0.01, 'intervention_idx': 0}
    _L2_gnn_all = _L2_gnn_setup()
    _L2_gnn_in = {k: v for k, v in _L2_gnn_all.items() if k in ('intervention_value', 'W1', 'b1', 'W2', 'b2')}
    del _L2_gnn_all

    def _L3_gnn_setup():
        import jax, jax.numpy as jnp
        import numpy as np
        ALPHA = 0.2
        THRESHOLD = 0.5
        NEG_INF = -9000000000000000.0
        key = jax.random.key(seed)
        k_in, k_adj, k_W, k_a = jax.random.split(key, 4)
        B, N, C = (32, 512, 64)
        inp = jax.random.normal(k_in, (B, N, C), dtype=jnp.float32)
        adj = jax.random.uniform(k_adj, (N, N), dtype=jnp.float32)
        gain = 1.414
        lim_W = gain * np.sqrt(6.0 / (C + C))
        W = jax.random.uniform(k_W, (C, C), dtype=jnp.float32, minval=-lim_W, maxval=lim_W)
        lim_a = gain * np.sqrt(6.0 / (2 * C + 1))
        a = jax.random.uniform(k_a, (2 * C, 1), dtype=jnp.float32, minval=-lim_a, maxval=lim_a)
        return {'input': inp, 'adj': adj, 'W': W, 'a': a}
    _L3_gnn_all = _L3_gnn_setup()
    _L3_gnn_in = {k: v for k, v in _L3_gnn_all.items() if k in ('W', 'a')}
    del _L3_gnn_all
    return {'x': x, 'adj': adj, 'L0_gnn_Wh': _L0_gnn_in['Wh'], 'L0_gnn_bh': _L0_gnn_in['bh'], 'L0_gnn_W_out': _L0_gnn_in['W_out'], 'L0_gnn_b_out': _L0_gnn_in['b_out'], 'L1_gnn_embedding': _L1_gnn_in['embedding'], 'L1_gnn_weight': _L1_gnn_in['weight'], 'L1_gnn_bias': _L1_gnn_in['bias'], 'L2_gnn_intervention_value': _L2_gnn_in['intervention_value'], 'L2_gnn_W1': _L2_gnn_in['W1'], 'L2_gnn_b1': _L2_gnn_in['b1'], 'L2_gnn_W2': _L2_gnn_in['W2'], 'L2_gnn_b2': _L2_gnn_in['b2'], 'L3_gnn_W': _L3_gnn_in['W'], 'L3_gnn_a': _L3_gnn_in['a']}

def reference(x, adj, L0_gnn_Wh, L0_gnn_bh, L0_gnn_W_out, L0_gnn_b_out, L1_gnn_embedding, L1_gnn_weight, L1_gnn_bias, L2_gnn_intervention_value, L2_gnn_W1, L2_gnn_b1, L2_gnn_W2, L2_gnn_b2, L3_gnn_W, L3_gnn_a):
    import jax
    import jax.numpy as jnp

    def _L0_gnn_ref(flow_x, graph, Wh, bh, W_out, b_out):
        import jax, jax.numpy as jnp
        import numpy as np
        NEG_INF = -1e+16

        def gat_layer(x, graph, W, b):
            h = x @ W
            s = jnp.einsum('bnd,bmd->bnm', h, h) * graph
            s = jnp.where(s == 0.0, NEG_INF, s)
            a = jax.nn.softmax(s, axis=2)
            return jnp.einsum('bnm,bmd->bnd', a, h) + b
        heads = jax.vmap(lambda W, b: gat_layer(flow_x, graph, W, b))(Wh, bh)
        H, B, N, D = heads.shape
        cat = jnp.moveaxis(heads, 0, 2).reshape(B, N, H * D)
        x = jax.nn.leaky_relu(cat, negative_slope=0.01)
        out = gat_layer(x, graph, W_out, b_out)
        return jax.nn.leaky_relu(out, negative_slope=0.01)

    def _L1_gnn_ref(x, A, embedding, weight, bias):
        import jax, jax.numpy as jnp
        import numpy as np
        K = weight.shape[1]
        N = A.shape[-2]
        w = jnp.einsum('nd,dkio->nkio', embedding, weight)
        b = jnp.einsum('nd,do->no', embedding, bias)
        As = [jnp.eye(N, dtype=x.dtype)]
        if K > 1:
            As.append(A)
        for _ in range(2, K):
            As.append(2.0 * (A @ As[-1]) - As[-2])
        A_stack = jnp.stack(As, 0)
        x_g = jnp.einsum('knm,bmc->bnkc', A_stack, x)
        out = jnp.einsum('bnki,nkio->bno', x_g, w)
        return out + b

    def _L2_gnn_ref(causal_vars, adj_matrix, intervention_value, W1, b1, W2, b2, intervention_idx):
        import jax, jax.numpy as jnp
        import numpy as np
        MAX_STEPS = 3
        v = causal_vars.at[:, intervention_idx].set(intervention_value)
        for _ in range(MAX_STEPS):
            effects = jnp.einsum('nm,bmd->bnd', adj_matrix, v)
            h = jnp.concatenate([v, effects], axis=-1)
            h = jax.nn.relu(jnp.einsum('bnk,dk->bnd', h, W1) + b1)
            v = jnp.einsum('bnk,dk->bnd', h, W2) + b2
        return v

    def _L3_gnn_ref(input, adj, W, a):
        import jax, jax.numpy as jnp
        import numpy as np
        ALPHA = 0.2
        THRESHOLD = 0.5
        NEG_INF = -9000000000000000.0
        h = jnp.matmul(input, W)
        C = W.shape[0]
        a_src = a[:C, 0]
        a_dst = a[C:, 0]
        s_src = jnp.matmul(h, a_src)
        s_dst = jnp.matmul(h, a_dst)
        e = jax.nn.leaky_relu(s_src[:, :, None] + s_dst[:, None, :], negative_slope=ALPHA)
        mask = adj > THRESHOLD
        attention = jax.nn.softmax(jnp.where(mask[None, :, :], e, NEG_INF), axis=2)
        h_prime = jnp.matmul(attention, h)
        return jax.nn.elu(h_prime)
    x = _layernorm(x + _L0_gnn_ref(x, adj, L0_gnn_Wh, L0_gnn_bh, L0_gnn_W_out, L0_gnn_b_out), axis=-1)
    x = _layernorm(x + _L1_gnn_ref(x, adj, L1_gnn_embedding, L1_gnn_weight, L1_gnn_bias), axis=-1)
    x = _layernorm(x + _L2_gnn_ref(x, adj, L2_gnn_intervention_value, L2_gnn_W1, L2_gnn_b1, L2_gnn_W2, L2_gnn_b2, 0), axis=-1)
    x = _layernorm(x + _L3_gnn_ref(x, adj, L3_gnn_W, L3_gnn_a), axis=-1)
    return x

_drawn_inputs = setup_inputs


def setup_inputs(seed=0):
    import zlib

    import numpy as np

    out = dict(_drawn_inputs(seed))
    spreads = {}
    factors = {'L0_gnn_b_out': 27.097,
     'L1_gnn_bias': 185.553,
     'L2_gnn_intervention_value': 21.438,
     'L2_gnn_b1': 21.46,
     'L2_gnn_b2': 8.0,
     'L3_gnn_a': 3.881}
    for name, (base, spread) in spreads.items():
        noise = np.random.default_rng([zlib.crc32(name.encode()), seed]).standard_normal(out[name].shape)
        drawn = base * np.exp(spread * noise) if base else spread * noise
        out[name] = jnp.asarray(drawn.astype(out[name].dtype))
    for name, factor in factors.items():
        out[name] = (out[name] * factor).astype(out[name].dtype)
    return out
```

```python
from contextlib import ExitStack

import concourse.bass as bass
from concourse import mybir

F32 = mybir.dt.float32
F32R = mybir.dt.float32r
ALU = mybir.AluOpType
ACT = mybir.ActivationFunctionType
AX = mybir.AxisListType

P = 128
B = 8
N = 1024
C = 64
HEADS = 8
HID = 128
NT = N // P
HALF = N // 2
PAIRS = B // 2
TPH = NT // 2
EMB = 16
ORDERS = 3
STEPS = 3
LEAK_HEADS = 0.01
NEG_HEADS = -1e16
NEG_EDGES = -9000000000000000.0
BIG = 3.0e38
EPS = 1e-5


def wait_count(engine, sem, value):
    if isinstance(value, int) and value <= 0:
        return
    engine.wait_ge(sem, value)


def wait_apart(engine, sem, value, passed):
    if isinstance(value, int):
        wait_count(engine, sem, value)
    else:
        engine.wait_ge(sem, value)
        engine.sem_inc(passed, 1)


def at(base, index, size):
    if isinstance(index, int):
        return slice(base + index * size, base + (index + 1) * size)
    return bass.ds(index * size + base, size)


def constants(nc, ctx, adj):
    def sb(name, shape, dt=F32):
        return ctx.enter_context(nc.sbuf_tensor(name, shape, dt))

    k = {
        "ident": sb("ident", [P, P]),
        "dup0": sb("dup0", [P, P]),
        "dup1": sb("dup1", [P, P]),
        "dups": sb("dups", [P, P]),
        "dups_r": sb("dups_r", [P, P], F32R),
        "graph": sb("graph", [P, NT, N]),
    }
    with ExitStack() as local:
        def sem(name):
            return local.enter_context(nc.semaphore(name))
        cleared, ident_made, dup_made, graph_in = sem("cleared"), sem("ident_made"), sem("dup_made"), sem("graph_in")
        block = local.enter_context(nc.Block())

        @block.sync
        def _(sync):
            sync.dma_start(k["graph"][:, :, :], adj.rearrange("(t p) m -> p t m", p=P)).then_inc(graph_in, 16)
            sync.wait_ge(graph_in, 16)

        @block.gpsimd
        def _(pool):
            pool.memset(k["ident"][:, :], 0.0).then_inc(cleared, 1)
            pool.wait_ge(cleared, 1)
            pool.affine_select(out=k["ident"][:, :], in_=k["ident"][:, :], compare_op=ALU.not_equal, fill=1.0,
                               base=0, pattern=[[-1, P]], channel_multiplier=1).then_inc(ident_made, 1)

        @block.vector
        def _(dve):
            dve.wait_ge(ident_made, 1)
            for col in (0, C):
                dve.tensor_copy(k["dup0"][:, col:col + C], k["ident"][:, 0:C]).then_inc(dup_made, 1)
                dve.tensor_copy(k["dup1"][:, col:col + C], k["ident"][:, C:P]).then_inc(dup_made, 1)
            dve.wait_ge(dup_made, 4)
            for dups in ("dups", "dups_r"):
                dve.tensor_tensor(k[dups][:, :], k["dup0"][:, :], k["dup1"][:, :], ALU.add)
    return k


def stack_parts(block, k, source, stacked, banks, ready, stacked_mm, high_in, low_in):
    slots = len(banks)

    @block.tensor
    def _(pe):
        ready(pe)
        for n in range(2 * B):
            moving, copies = source(n // 2, n % 2)
            wait_count(pe, low_in, n - slots + 1)
            pe.matmul(banks[n % slots], copies, moving, start=True, stop=True).then_inc(stacked_mm, 1)

    @block.scalar
    def _(act):
        for n in range(2 * B):
            act.wait_ge(stacked_mm, n + 1)
            act.activation(stacked[:, n // 2, at(0, n % 2, HALF)], banks[n % slots], ACT.Copy).then_inc(high_in, 1)

    @block.vector
    def _(dve):
        for n in range(2 * B):
            low = stacked[C:P, n // 2, at(0, n % 2, HALF)]
            dve.wait_ge(high_in, n + 1)
            dve.tensor_tensor(low, banks[n % slots][C:P, :], low.bitcast(F32), ALU.subtract).then_inc(low_in, 1)


def prepare_heads(nc, k, x, Wh, bh, W_out, xs, head_gram, head_w, out_w, head_b, sums):
    with ExitStack() as local:
        def sb(name, shape, dt=F32):
            return local.enter_context(nc.sbuf_tensor(name, shape, dt))

        def sem(name):
            return local.enter_context(nc.semaphore(name))

        x_nat = sb("x_nat", [P, NT, B * C])
        x_pairs = sb("x_pairs", [P, PAIRS, N])
        wt = sb("wt", [P, HEADS, P])
        banks = [local.enter_context(nc.psum_tensor(f"ph{i}", [P, HALF], F32))[:, :] for i in range(8)]
        w_in, x_in, turned, taken = sem("w_in"), sem("x_in"), sem("turned"), sem("taken")
        stacked_mm, high_in, low_in = sem("stacked_mm"), sem("high_in"), sem("low_in")
        block = local.enter_context(nc.Block())
        W_BANKS = HEADS // 4

        @block.sync
        def _(sync):
            for copy in (0, C):
                sync.dma_start(head_w[copy:copy + C, :, :], Wh.rearrange("h c d -> c h d")).then_inc(w_in, 16)
            sync.dma_start(out_w[:, :, :], W_out.rearrange("(h d) o -> d h o", d=HID)).then_inc(w_in, 16)
            sync.dma_start(head_b[:, :, 0], bh.rearrange("h d -> d h"), allow_slow_non_contiguous=True).then_inc(w_in, 16)
            xv = x.rearrange("b (t p) c -> p t b c", p=P)
            for t in range(NT):
                sync.dma_start(x_nat[:, t, :].rearrange("p (b c) -> p b c", b=B), xv[:, t]).then_inc(x_in, 16)

        @block.gpsimd
        def _(pool):
            pool.memset(sums[:, :, :], 0.0)

        @block.tensor
        def _(pe):
            pe.wait_ge(w_in, 64)
            for h in range(HEADS):
                last = pe.transpose(banks[h // 4][:, at(0, h % 4, P)], head_w[:, h, :], k["ident"][:, :])
                if h % 4 == 3:
                    last.then_inc(turned, 1)
            pe.wait_ge(x_in, 16 * NT)
            for g in range(PAIRS * 2):
                bank = banks[(W_BANKS + g) % 8]
                wait_count(pe, taken, W_BANKS + g - 7)
                for t in range(TPH):
                    last = pe.transpose(bank[:, at(0, t, P)], x_nat[:, (g % 2) * TPH + t, at(0, g // 2, P)],
                                        k["ident"][:, :])
                last.then_inc(turned, 1)
            pe.wait_ge(taken, W_BANKS + 2 * PAIRS)
            for h in range(HEADS):
                last = pe.matmul(banks[h // 4][:, at(0, h % 4, P)], wt[:, h, :], wt[:, h, :], start=True, stop=True)
                if h % 4 == 3:
                    last.then_inc(turned, 1)

        @block.vector
        def _(dve):
            dve.wait_ge(w_in, 64)
            dve.tensor_scalar(head_b[:, :, 1], head_b[:, :, 0], -LEAK_HEADS, None, ALU.mult)
            for g in range(W_BANKS + 2 * PAIRS):
                dve.wait_ge(turned, g + 1)
                if g < W_BANKS:
                    out = wt[:, 4 * g:4 * g + 4, :]
                    dve.tensor_copy(out, banks[g].rearrange("p (h d) -> p h d", h=4)).then_inc(taken, 1)
                else:
                    q = g - W_BANKS
                    dve.tensor_copy(x_pairs[:, q // 2, at(0, q % 2, HALF)], banks[g % 8]).then_inc(taken, 1)
            for g in range(W_BANKS):
                dve.wait_ge(turned, W_BANKS + 2 * PAIRS + g + 1)
                high, low = (head_gram[:, 4 * g:4 * g + 4, part, :] for part in range(2))
                gram = banks[g].rearrange("p (h d) -> p h d", h=4)
                dve.tensor_copy(high, gram).then_inc(taken, 1)
                dve.wait_ge(taken, W_BANKS + 2 * PAIRS + 2 * g + 1)
                dve.tensor_tensor(low, gram, high.bitcast(F32), ALU.subtract).then_inc(taken, 1)

        stack_parts(block, k,
                    lambda b, half: (x_pairs[:, b // 2, at(0, half, HALF)], k[f"dup{b % 2}"][:, :]),
                    xs, banks[4:8], lambda pe: pe.wait_ge(taken, 3 * W_BANKS + 2 * PAIRS),
                    stacked_mm, high_in, low_in)


def prepare_output_head(nc, k, sums, xs, nat):
    with ExitStack() as local:
        def sem(name):
            return local.enter_context(nc.semaphore(name))

        banks = [local.enter_context(nc.psum_tensor(f"po{i}", [P, HALF], F32))[:, :] for i in range(8)]
        turned, taken = sem("turned2"), sem("taken2")
        stacked_mm, high_in, low_in = sem("stacked_mm2"), sem("high_in2"), sem("low_in2")
        block = local.enter_context(nc.Block())

        @block.tensor
        def _(pe):
            for b in range(B):
                wait_count(pe, taken, b - 3)
                for t in range(TPH):
                    last = pe.transpose(banks[b % 4][:, at(0, t, P)], sums[:, b, at(0, t, P)], k["ident"][:, :])
                last.then_inc(turned, 1)

        @block.vector
        def _(dve):
            for b in range(B):
                dve.wait_ge(turned, b + 1)
                dve.tensor_copy(nat[:, :, b, :].rearrange("p (h t) c -> p t h c", h=2),
                                banks[b % 4].rearrange("p (t h c) -> p t h c", t=TPH, h=2)).then_inc(taken, 1)

        stack_parts(block, k, lambda b, half: (sums[:, b, :], k[f"dup{half}"][:, :]),
                    xs, banks[4:8], lambda pe: None, stacked_mm, high_in, low_in)


def prepare_edges(nc, k, x_cur, W, a, nat, src_score, dst_w, x_pairs):
    with ExitStack() as local:
        def sb(name, shape, dt=F32):
            return local.enter_context(nc.sbuf_tensor(name, shape, dt))

        def sem(name):
            return local.enter_context(nc.semaphore(name))

        WIDE = P + 2
        w2 = sb("w2", [P, WIDE])
        w2t = sb("w2t", [P, P])
        a4 = sb("a4", [P, 4])
        wa = sb("wa", [P, 4])
        ones = sb("ones", [P, P])
        banks = [local.enter_context(nc.psum_tensor(f"pe{i}", [P, HALF], F32))[:, :] for i in range(8)]
        cleared, w_in, turned, taken, made = sem("cleared4"), sem("w_in4"), sem("turned4"), sem("taken4"), sem("made4")
        h_mm, h_in, masked = sem("h_mm"), sem("h_in"), sem("masked4")
        block = local.enter_context(nc.Block())

        @block.sync
        def _(sync):
            sync.wait_ge(cleared, 2)
            for q in range(2):
                rows = slice(q * C, (q + 1) * C)
                sync.dma_start(w2[rows, q * C:(q + 1) * C], W).then_inc(w_in, 16)
                sync.dma_start(a4[rows, q:q + 1], a[0:C, :]).then_inc(w_in, 16)
                sync.dma_start(a4[rows, 2 + q:3 + q], a[C:2 * C, :]).then_inc(w_in, 16)

        @block.gpsimd
        def _(pool):
            pool.memset(w2[:, :], 0.0).then_inc(cleared, 1)
            pool.memset(a4[:, :], 0.0).then_inc(cleared, 1)
            pool.memset(ones[:, :], 1.0).then_inc(cleared, 1)

        @block.tensor
        def _(pe):
            pe.wait_ge(w_in, 96)
            pe.transpose(banks[0][:, 0:P], w2[:, 0:P], k["ident"][:, :]).then_inc(turned, 1)
            for g in range(2 * PAIRS):
                bank = banks[(1 + g) % 8]
                wait_count(pe, taken, g - 6)
                for t in range(TPH):
                    last = pe.transpose(bank[:, at(0, t, P)], x_cur[:, (g % 2) * TPH + t, at(0, g // 2, P)],
                                        k["ident"][:, :])
                last.then_inc(turned, 1)
            pe.wait_ge(taken, 1 + 2 * PAIRS)
            pe.matmul(banks[0][:, 0:4], w2t[:, :], a4[:, :], start=True, stop=True).then_inc(turned, 1)
            pe.wait_ge(made, 1)
            for n in range(PAIRS * NT):
                wait_count(pe, h_in, n - 3)
                pe.matmul(banks[1 + n % 4][:, 0:WIDE], x_pairs[:, n // NT, at(0, n % NT, P)], w2[:, :],
                          start=True, stop=True).then_inc(h_mm, 1)

        @block.vector
        def _(dve):
            dve.wait_ge(turned, 1)
            dve.tensor_copy(w2t[:, :], banks[0][:, 0:P]).then_inc(taken, 1)
            for g in range(2 * PAIRS):
                dve.wait_ge(turned, g + 2)
                dve.tensor_copy(x_pairs[:, g // 2, at(0, g % 2, HALF)], banks[(1 + g) % 8]).then_inc(taken, 1)
            dve.wait_ge(turned, 2 + 2 * PAIRS)
            dve.tensor_copy(wa[:, :], banks[0][:, 0:4]).then_inc(taken, 1)
            dve.wait_ge(taken, 2 + 2 * PAIRS)
            dve.tensor_copy(w2[:, P:WIDE], wa[:, 0:2]).then_inc(made, 1)
            dve.wait_ge(cleared, 3)
            for q in range(2):
                dve.tensor_scalar(dst_w[:, q, :], ones[:, :], wa[:, 2 + q:3 + q], None, ALU.mult)
            for t in range(NT):
                dve.tensor_scalar(k["graph"][:, t, :], k["graph"][:, t, :], 0.5, NEG_EDGES, ALU.is_le, ALU.mult)

        @block.scalar
        def _(act):
            for n in range(PAIRS * NT):
                pair, t = n // NT, n % NT
                bank = banks[1 + n % 4]
                act.wait_ge(h_mm, n + 1)
                act.activation(nat[:, t, 2 * pair:2 * pair + 2, :],
                               bank[:, 0:P].rearrange("p (b c) -> p b c", b=2), ACT.Copy)
                act.activation(src_score[:, 2 * pair:2 * pair + 2, t], bank[:, P:WIDE], ACT.Copy).then_inc(h_in, 1)


QUERY_TURN = 7
HEAD_UNITS, OUTPUT_UNITS, EDGE_UNITS = "heads", "output", "edges"
LAG_EXP, LAG_RECIP, LAG_TURN = 1, 2, 3


def attention(nc, k, kind, values, res, xs=None, head_gram=None, head_w=None, out_w=None, head_b=None,
              src_score=None, dst_w=None, x_pairs=None):
    units = B * HEADS if kind == HEAD_UNITS else B
    split = kind != EDGE_UNITS

    def batch(U):
        return U // HEADS if kind == HEAD_UNITS else U

    with ExitStack() as local:
        def sb(name, shape, dt=F32):
            return local.enter_context(nc.sbuf_tensor(f"{kind}_{name}", shape, dt))

        def psum(name, shape):
            return local.enter_context(nc.psum_tensor(f"{kind}_{name}", shape, F32))

        def sem(name):
            return local.enter_context(nc.semaphore(f"{kind}_{name}"))

        S = psum("S", [P, 2, N])
        turn = psum("turn", [P, 2, HALF])
        mix = psum("mix", [P, HALF])
        back = psum("back", [P, HALF])

        prod = sb("prod", [P, 2, N])
        floor = sb("floor", [P, 2, N], mybir.dt.bfloat16 if split else F32)
        neg = sb("neg", [P, 2, N])
        e = sb("e", [P, 4, N])
        neg_max = sb("neg_max", [P, 2, NT])
        row_sum = sb("row_sum", [P, 2, NT])
        row_inv = sb("row_inv", [P, 2, NT])
        weights_t = sb("weights_t", [P, 2, NT, HALF])
        val = [sb(f"val{i}", [P, NT, C]) for i in range(2)]
        mixed = [sb(f"mixed{i}", [P, HALF]) for i in range(2)]
        if split:
            q_high = [sb(f"q_high{i}", [P, N], F32R) for i in range(2)]
            q_low = [sb(f"q_low{i}", [P, N], F32R) for i in range(2)]
        else:
            dst = sb("dst", [P, 2, N])
            src = sb("src", [P, 2, NT])
        if kind == HEAD_UNITS:
            gram = [sb(f"gram{i}", [P, 2, P], F32R) for i in range(2)]
            w_now = [sb(f"w_now{i}", [P, HID]) for i in range(2)]
            ow_now = [sb(f"ow_now{i}", [P, C]) for i in range(2)]
            b_now = [sb(f"b_now{i}", [P, 2]) for i in range(2)]
            above = [sb(f"above{i}", [P, HALF]) for i in range(2)]
            below = [sb(f"below{i}", [P, HALF]) for i in range(2)]
            cat = [sb(f"cat{i}", [P, HALF]) for i in range(2)]

        val_in = [sem(f"val_in{i}") for i in range(2)]
        if split:
            q_mm, q_high_in, q_low_in, scored = sem("q_mm"), sem("q_high_in"), sem("q_low_in"), sem("scored")
        else:
            dst_mm, dst_in, src_in = sem("dst_mm"), sem("dst_in"), sem("src_in")
        if kind == HEAD_UNITS:
            gram_in, back_in = sem("gram_in"), sem("back_in")
            head_mm, biased, cat_in = sem("head_mm"), sem("biased"), sem("cat_in")
        prod_in, floor_in, max_in = sem("prod_in"), sem("floor_in"), sem("max_in")
        exp_in, inv_in, normed = sem("exp_in"), sem("inv_in"), sem("normed")
        turned, turned_in = sem("turned"), sem("turned_in")
        mixed_mm, mixed_in = sem("mixed_mm"), sem("mixed_in")
        out_mm, out_in = sem("out_mm"), sem("out_in")
        dve_passed, pool_passed = sem("dve_passed"), sem("pool_passed")
        block = local.enter_context(nc.Block())

        def run(engine, unit, tail):
            unit(0, 0, None)
            with engine.Fori(1, units - 2, 2) as U:
                unit(U, 1, U - 1)
                unit(U + 1, 0, U)
            unit(units - 1, 1, units - 2)
            tail(units - 1)

        def lagged(U, V, s, lag):
            return (U, True, s - lag) if s >= lag else (V, False, s - lag + NT)

        def slot_of(u, i):
            return (u + i + (i >= QUERY_TURN)) % 2

        def query_slot(w):
            return (1 - w + QUERY_TURN) % 2

        @block.tensor
        def _(pe):
            def queries(W, w):
                if not split:
                    return
                slot = S[:, query_slot(w), :]
                if kind == HEAD_UNITS:
                    pe.wait_ge(gram_in, W + 1)
                wait_count(pe, prod_in, (W - 1) * NT + QUERY_TURN - 1)
                parts = [gram[w][:, part, :] for part in range(2)] if kind == HEAD_UNITS else [k["dups_r"][:, :]]
                for n, part in enumerate(parts):
                    for half in range(2):
                        last = pe.matmul(slot[:, at(0, half, HALF)], part, xs[:, batch(W), at(0, half, HALF)],
                                         start=n == 0, stop=n == len(parts) - 1)
                last.then_inc(q_mm, 1)

            def destinations(W, w, q):
                wait_count(pe, dst_in, W - 1)
                for half in range(2):
                    last = pe.matmul(S[:, w, at(0, half, HALF)], dst_w[:, q, :],
                                     x_pairs[:, W // 2, at(0, half, HALF)], start=True, stop=True)
                last.then_inc(dst_mm, 1)

            def scores(U, u, i):
                if not split:
                    return
                if i == 0:
                    pe.wait_ge(q_low_in, U + 1)
                wait_count(pe, prod_in, U * NT + (i if i == QUERY_TURN else i - 1))
                for n, part in enumerate((q_high, q_low)):
                    for half in range(2):
                        last = pe.matmul(S[:, slot_of(u, i), at(0, half, HALF)], part[u][:, at(0, i, P)],
                                         xs[:, batch(U), at(0, half, HALF)], start=n == 0, stop=n == 1)
                last.then_inc(scored, 1)

            def transposes(V, i):
                T = V * NT + i
                pe.wait_ge(normed, T + 1)
                for g in range(2):
                    wait_count(pe, turned_in, 2 * T + g - 1)
                    for j in range(TPH):
                        last = pe.transpose(turn[:, g, at(0, j, P)], e[:, i % 4, at(0, g * TPH + j, P)],
                                            k["ident"][:, :])
                    last.then_inc(turned, 1)

            def mixing(V, v, half, first, end):
                if first == 0:
                    pe.wait_ge(turned_in, 2 * (V * NT + (half + 1) * TPH))
                    if half == 0:
                        pe.wait_ge(val_in[v], 16 * (V // 2 + 1))
                for t in range(first, end):
                    rows = slice(C * (t % 2), C * (t % 2) + C)
                    last = pe.matmul(mix[rows, :], val[v][:, t, :], weights_t[:, half, t, :],
                                     start=t < 2, stop=t >= NT - 2)
                if end == NT:
                    last.then_inc(mixed_mm, 1)

            def after(V, v, half):
                n = 2 * V + half
                pe.wait_ge(mixed_in, n + 1)
                if kind == HEAD_UNITS:
                    if half == 0:
                        pe.wait_ge(back_in, V + 1)
                        pe.wait_ge(out_in, V + 1)
                    else:
                        pe.wait_ge(biased, n)
                    pe.matmul(back[:, :], w_now[v][:, :], mixed[half][:, :], start=True, stop=True).then_inc(head_mm, 1)
                else:
                    for t in range(TPH):
                        last = pe.matmul(back[:, at(0, t, C)], mixed[half][:, at(0, t, P)], k["dups"][:, 0:C],
                                         start=True, stop=True)
                    last.then_inc(out_mm, 1)

            def outputs(V, v):
                if kind != HEAD_UNITS:
                    return
                pe.wait_ge(cat_in, 2 * V + 2)
                for half in range(2):
                    last = pe.matmul(back[half * C:half * C + C, :], ow_now[v][:, :], cat[half][:, :],
                                     start=True, stop=True)
                last.then_inc(out_mm, 1)

            def behind(V, v, s):
                if s < 3:
                    mixing(V, v, 0, 2 * s + 2, 2 * s + 4)
                if s in (3, 4):
                    mixing(V, v, 1, (s - 3) * TPH, (s - 2) * TPH)
                if s == 7:
                    outputs(V, v)

            def behind_turned(V, v, s):
                if s == 2:
                    after(V, v, 0)
                if s == 5:
                    after(V, v, 1)

            def unit(U, u, V):
                more = not (isinstance(U, int) and U == units - 1)
                for s in range(NT):
                    scores(U, u, s)
                    if s == QUERY_TURN - 1 and more:
                        queries(U + 1, 1 - u)
                    if V is not None:
                        behind(V, 1 - u, s)
                    W, _, i = lagged(U, V, s, LAG_TURN)
                    if W is not None:
                        transposes(W, i)
                    if V is not None:
                        behind_turned(V, 1 - u, s)
                    if s == NT - 1:
                        mixing(U, u, 0, 0, 2)
                    if s == 2 and more and not split:
                        destinations(U + 1, 1 - u, 1 - u)

            queries(0, 0)
            if not split:
                destinations(0, 0, 0)

            def tail(V):
                for s in range(NT):
                    behind(V, 1, s)
                    if s < LAG_TURN:
                        transposes(V, s - LAG_TURN + NT)
                    behind_turned(V, 1, s)
            run(pe, unit, tail)

        @block.vector
        def _(dve):
            def masking(U, u, i):
                T = U * NT + i
                wait_count(dve, max_in, T - 1)
                if split:
                    dve.wait_ge(scored, T + 1)
                    dve.tensor_tensor(prod[:, i % 2, :], S[:, slot_of(u, i), :], k["graph"][:, i, :],
                                      ALU.mult).then_inc(prod_in, 1)
                else:
                    if i == 0:
                        dve.wait_ge(dst_in, U + 1)
                        dve.tensor_copy(src[:, u, :], src_score[:, batch(U), :] if isinstance(U, int) else
                                        src_score[:, bass.ds(U, 1), :].rearrange("p a t -> p (a t)")).then_inc(src_in, 1)
                        dve.wait_ge(src_in, U + 1)
                    dve.tensor_scalar(prod[:, i % 2, :], dst[:, u, :], src[:, u, i:i + 1], None,
                                      ALU.add).then_inc(prod_in, 1)

            def flooring(U, i):
                T = U * NT + i
                dve.wait_ge(prod_in, T + 1)
                wait_count(dve, max_in, T - 1)
                if split:
                    dve.tensor_scalar(floor[:, i % 2, :], prod[:, i % 2, :], 0.0, NEG_HEADS,
                                      ALU.is_equal, ALU.mult).then_inc(floor_in, 1)
                else:
                    dve.scalar_tensor_tensor(out=floor[:, i % 2, :], in0=prod[:, i % 2, :], scalar=0.2,
                                             in1=prod[:, i % 2, :], op0=ALU.mult, op1=ALU.max).then_inc(floor_in, 1)

            def maximum(V, v, i):
                T = V * NT + i
                wait_count(dve, floor_in, T + 1)
                wait_apart(dve, exp_in, T - 1, dve_passed)
                if split:
                    in0, in1 = prod[:, i % 2, :], floor[:, i % 2, :]
                else:
                    in0, in1 = floor[:, i % 2, :], k["graph"][:, i, :]
                dve.tensor_tensor_reduce(neg[:, i % 2, :], in0, in1, -1.0, BIG, ALU.add, ALU.min,
                                         neg_max[:, v, i:i + 1]).then_inc(max_in, 1)

            def inverse(V, v, i):
                dve.wait_ge(exp_in, V * NT + i + 1)
                dve.reciprocal(row_inv[:, v, i:i + 1], row_sum[:, v, i:i + 1]).then_inc(inv_in, 1)

            def low_part(W, w):
                if not split:
                    return
                dve.wait_ge(q_high_in, W + 1)
                dve.tensor_tensor(q_low[w][:, :], S[:, query_slot(w), :], q_high[w][:, :].bitcast(F32),
                                  ALU.subtract).then_inc(q_low_in, 1)

            def add_heads(V):
                if kind != HEAD_UNITS:
                    return
                dve.wait_ge(out_mm, V + 1)
                dve.wait_ge(out_in, V + 1)
                dve.tensor_tensor(res[:, batch(V), :], res[:, batch(V), :], back[:, :], ALU.add).then_inc(out_in, 1)

            def unit(U, u, V):
                for s in range(NT):
                    masking(U, u, s)
                    W, same, i = lagged(U, V, s, LAG_RECIP)
                    if W is not None:
                        inverse(W, u if same else 1 - u, i)
                    W, same, i = lagged(U, V, s, LAG_EXP)
                    if W is not None:
                        maximum(W, u if same else 1 - u, i)
                    if s == QUERY_TURN and not (isinstance(U, int) and U == units - 1):
                        low_part(U + 1, 1 - u)
                    flooring(U, s)
                    if s == 7 and V is not None:
                        add_heads(V)

            if kind == HEAD_UNITS:
                dve.memset(res[:, :, :], 0.0).then_inc(out_in, 1)
            low_part(0, 0)

            def tail(V):
                for s in range(LAG_RECIP):
                    if s == 0:
                        maximum(V, 1, NT - 1)
                    inverse(V, 1, s - LAG_RECIP + NT)
                add_heads(V)
            run(dve, unit, tail)

        @block.scalar
        def _(act):
            def exponent(V, v, i):
                T = V * NT + i
                act.wait_ge(max_in, T + 1)
                wait_count(act, turned, 2 * (T - 3))
                act.activation(e[:, i % 4, :], neg[:, i % 2, :], ACT.Exp, bias=neg_max[:, v, i:i + 1],
                               scale=-1.0, accum_out=row_sum[:, v, i:i + 1]).then_inc(exp_in, 1)

            def take_turned(V, i):
                T, half = V * NT + i, i // TPH
                for g in range(2):
                    act.wait_ge(turned, 2 * T + g + 1)
                    act.activation(weights_t[:, half, g * TPH:(g + 1) * TPH, at(0, i % TPH, P)],
                                   turn[:, g, :].rearrange("p (t n) -> p t n", t=TPH), ACT.Copy).then_inc(turned_in, 1)

            def high_part(W, w):
                if not split:
                    return
                act.wait_ge(q_mm, W + 1)
                act.activation(q_high[w][:, :], S[:, query_slot(w), :], ACT.Copy).then_inc(q_high_in, 1)

            def take_destinations(W, w):
                if split:
                    return
                act.wait_ge(dst_mm, W + 1)
                wait_count(act, prod_in, (W - 1) * NT)
                act.activation(dst[:, w, :], S[:, w, :], ACT.Copy).then_inc(dst_in, 1)

            def take_mixed(V, half):
                act.wait_ge(mixed_mm, 2 * V + half + 1)
                act.activation(mixed[half][:, :], mix[:, :], ACT.Copy).then_inc(mixed_in, 1)

            def take_back(V, v, half):
                n = 2 * V + half
                if kind == HEAD_UNITS:
                    act.wait_ge(head_mm, n + 1)
                    act.activation(above[half][:, :], back[:, :], ACT.Relu, bias=b_now[v][:, 0:1])
                    act.activation(below[half][:, :], back[:, :], ACT.Relu, bias=b_now[v][:, 1:2],
                                   scale=-LEAK_HEADS).then_inc(biased, 1)
                else:
                    act.wait_ge(out_mm, n + 1)
                    out = res[:, half * TPH:(half + 1) * TPH, V, :] if isinstance(V, int) else \
                        res[:, half * TPH:(half + 1) * TPH, bass.ds(V, 1), :].rearrange("p t a c -> p t (a c)")
                    act.activation(out, back[:, 0:TPH * C].rearrange("p (t c) -> p t c", t=TPH), ACT.Copy).then_inc(out_in, 1)

            def behind(V, v, s):
                if s == 2:
                    take_mixed(V, 0)
                if s == 3:
                    take_back(V, v, 0)
                if s == 5:
                    take_mixed(V, 1)
                if s == 6:
                    take_back(V, v, 1)

            def unit(U, u, V):
                for s in range(NT):
                    if V is not None:
                        behind(V, 1 - u, s)
                    more = not (isinstance(U, int) and U == units - 1)
                    if s == QUERY_TURN and more:
                        high_part(U + 1, 1 - u)
                    W, same, i = lagged(U, V, s, LAG_TURN)
                    if W is not None:
                        take_turned(W, i)
                    W, same, i = lagged(U, V, s, LAG_EXP)
                    if W is not None:
                        exponent(W, u if same else 1 - u, i)
                    if s == 3 and more:
                        take_destinations(U + 1, 1 - u)

            high_part(0, 0)
            take_destinations(0, 0)

            def tail(V):
                for s in range(NT):
                    behind(V, 1, s)
                    if s == 0:
                        exponent(V, 1, NT - 1)
                    if s < LAG_TURN:
                        take_turned(V, s - LAG_TURN + NT)
            run(act, unit, tail)

        @block.gpsimd
        def _(pool):
            def normalise(V, v, i):
                wait_apart(pool, inv_in, V * NT + i + 1, pool_passed)
                pool.tensor_scalar(e[:, i % 4, :], e[:, i % 4, :], row_inv[:, v, i:i + 1], 1.0,
                                   ALU.mult, ALU.mult).then_inc(normed, 1)

            def copy(out, source):
                return pool.tensor_copy(out, source)

            def of_head(tensor, U):
                return tensor[:, U % HEADS]

            def copy_gram(W, w):
                if kind == HEAD_UNITS:
                    wait_apart(pool, q_mm, W - 1, pool_passed)
                    copy(gram[w][:, :, :], of_head(head_gram, W)).then_inc(gram_in, 1)

            def copy_head(W, w):
                if kind == HEAD_UNITS:
                    wait_apart(pool, out_mm, W - 1, pool_passed)
                    copy(w_now[w][:, :], of_head(head_w, W))
                    copy(ow_now[w][:, :], of_head(out_w, W))
                    copy(b_now[w][:, :], of_head(head_b, W)).then_inc(back_in, 1)

            def leaky(V, half):
                if kind == HEAD_UNITS:
                    pool.wait_ge(biased, 2 * V + half + 1)
                    pool.tensor_tensor(cat[half][:, :], above[half][:, :], below[half][:, :],
                                       ALU.subtract).then_inc(cat_in, 1)

            def behind(V, s):
                if s == 4:
                    leaky(V, 0)
                if s == 7:
                    leaky(V, 1)

            def unit(U, u, V):
                for s in range(NT):
                    if V is not None:
                        behind(V, s)
                    W, same, i = lagged(U, V, s, LAG_RECIP)
                    if W is not None:
                        normalise(W, u if same else 1 - u, i)
                    if isinstance(U, int) and U == units - 1:
                        continue
                    if s == 0:
                        copy_gram(U + 1, 1 - u)
                    if s == 7:
                        copy_head(U + 1, 1 - u)

            copy_gram(0, 0)
            copy_head(0, 0)

            def tail(V):
                for s in range(NT):
                    if s < LAG_RECIP:
                        normalise(V, 1, s - LAG_RECIP + NT)
                    behind(V, s)
            run(pool, unit, tail)

        @block.sync
        def _(sync):
            def load(W, w):
                wait_count(sync, mixed_mm, 2 * (W - 1))
                sync.dma_start(val[w][:, :, :], values(batch(W))).then_inc(val_in[w], 16)
            load(0, 0)
            load(1, 1)
            with sync.Fori(2, units - 1, 2) as W:
                load(W, 0)
                load(W + 1, 1)


def layer_norm(nc, name, x_cur, res, finish, loads=()):
    GROUPS = 2
    ROWS = NT * B // GROUPS
    with ExitStack() as local:
        def sb(n, shape, dt=F32):
            return local.enter_context(nc.sbuf_tensor(f"{name}_{n}", shape, dt))

        def sem(n):
            return local.enter_context(nc.semaphore(f"{name}_{n}"))

        tmp = sb("tmp", [P, GROUPS, ROWS, C])
        mean = sb("mean", [P, GROUPS, ROWS])
        var = sb("var", [P, GROUPS, ROWS])
        std = sb("std", [P, GROUPS, ROWS])
        bias = sb("bias", [P, C])
        step, squared, rooted, centred = sem("step"), sem("squared"), sem("rooted"), sem("centred")
        if finish[0] == "elu":
            act_step, ready_for_exp = sem("act_step"), sem("ready_for_exp")
        if finish[0] == "leaky" or loads:
            loaded = sem("loaded")
        block = local.enter_context(nc.Block())
        rows = "p t b c -> p (t b) c"
        per = NT // GROUPS
        X = [x_cur[:, g * per:(g + 1) * per].rearrange(rows) for g in range(GROUPS)]
        R = [res[:, g * per:(g + 1) * per].rearrange(rows) for g in range(GROUPS)]

        def wide(a):
            return a.unsqueeze(2).broadcast_to([P, ROWS, C])

        @block.sync
        def _(sync):
            for out, source in [l for l in loads] + ([(bias[:, :], finish[1])] if finish[0] == "leaky" else []):
                sync.dma_start(out, source).then_inc(loaded, 16)

        n_loads = len(loads) + (finish[0] == "leaky")

        @block.vector
        def _(dve):
            count = [0]

            def then(ins):
                count[0] += 1
                ins.then_inc(step, 1)
                dve.wait_ge(step, count[0])

            if n_loads:
                dve.wait_ge(loaded, 16 * n_loads)
            for g in range(GROUPS):
                if finish[0] == "leaky":
                    then(dve.tensor_tensor(R[g], R[g], bias[:, :].unsqueeze(1).broadcast_to([P, ROWS, C]), ALU.add))
                    then(dve.scalar_tensor_tensor(out=R[g], in0=R[g], scalar=0.01, in1=R[g], op0=ALU.mult, op1=ALU.max))
                if finish[0] == "elu":
                    then(dve.tensor_scalar(tmp[:, g], R[g], 0.0, None, ALU.min))
                    dve.sem_inc(ready_for_exp, 1)
                    dve.wait_ge(act_step, g + 1)
                    then(dve.scalar_tensor_tensor(out=R[g], in0=R[g], scalar=0.0, in1=tmp[:, g], op0=ALU.max, op1=ALU.add))
                    then(dve.tensor_scalar(R[g], R[g], -1.0, None, ALU.add))
                then(dve.tensor_tensor(X[g], X[g], R[g], ALU.add))
                then(dve.tensor_reduce(mean[:, g], X[g], AX.X, ALU.add))
                then(dve.tensor_scalar(mean[:, g], mean[:, g], 1.0 / C, None, ALU.mult))
                then(dve.tensor_tensor(X[g], X[g], wide(mean[:, g]), ALU.subtract))
                dve.sem_inc(centred, 1)
                dve.wait_ge(squared, g + 1)
                then(dve.tensor_reduce(var[:, g], tmp[:, g], AX.X, ALU.add))
                then(dve.tensor_scalar(var[:, g], var[:, g], 1.0 / C, EPS, ALU.mult, ALU.add))
            for g in range(GROUPS):
                dve.wait_ge(rooted, g + 1)
                then(dve.reciprocal(std[:, g], std[:, g]))
                then(dve.tensor_tensor(X[g], X[g], wide(std[:, g]), ALU.mult))

        @block.scalar
        def _(act):
            for g in range(GROUPS):
                if finish[0] == "elu":
                    act.wait_ge(ready_for_exp, g + 1)
                    act.activation(tmp[:, g], tmp[:, g], ACT.Exp).then_inc(act_step, 1)
                act.wait_ge(centred, g + 1)
                act.activation(tmp[:, g], X[g], ACT.Square).then_inc(squared, 1)
            per_group = {"leaky": 2, "elu": 3, "none": 0}[finish[0]] + 6
            for g in range(GROUPS):
                act.wait_ge(step, per_group * (g + 1))
                act.activation(std[:, g], var[:, g], ACT.Sqrt).then_inc(rooted, 1)


def chebyshev(nc, k, x_cur, res, graph_t, embedding, weight, bias):
    with ExitStack() as local:
        def sb(name, shape, dt=F32):
            return local.enter_context(nc.sbuf_tensor(name, shape, dt))

        def sem(name):
            return local.enter_context(nc.semaphore(name))

        t1 = sb("t1", [P, NT, B * C])
        t2 = sb("t2", [P, NT, B * C])
        emb = sb("emb", [P, NT, EMB])
        w01 = sb("w01", [P, EMB, C])
        w2b = sb("w2b", [P, EMB, C])
        joined = [sb(f"joined{i}", [P, B, 4, C]) for i in range(2)]
        joined_t = [sb(f"joined_t{i}", [P, 4, P]) for i in range(2)]
        prods = sb("prods", [P, 2, EMB, C])
        banks = [local.enter_context(nc.psum_tensor(f"pc{i}", [P, HALF], F32))[:, :] for i in range(4)]
        y = local.enter_context(nc.psum_tensor("cheb_y", [P, 2, EMB * C], F32))
        w_in, cleared, g_turned, g_in = sem("w_inc"), sem("clearedc"), sem("g_turned"), sem("g_inc")
        t_mm, t_in = sem("t_mm"), sem("t_in")
        join_in, join_mm, join_t_in = sem("join_in"), sem("join_mm"), sem("join_t_in")
        y_mm, prod_in, sum_in = sem("y_mm"), sem("prod_inc"), sem("sum_in")
        pool_passed = sem("pool_passedc")
        block = local.enter_context(nc.Block())
        G_BANKS = NT * 2

        @block.sync
        def _(sync):
            sync.wait_ge(cleared, 1)
            sync.dma_start(emb[:, :, :], embedding.rearrange("(t p) d -> p t d", p=P)).then_inc(w_in, 16)
            for order in range(ORDERS):
                out = w01[order * C:(order + 1) * C, :, :] if order < 2 else w2b[0:C, :, :]
                sync.dma_start(out, weight[:, order].rearrange("d i o -> i d o")).then_inc(w_in, 16)
            sync.dma_start(w2b[C:C + 1, :, :], bias.unsqueeze(0)).then_inc(w_in, 16)

        @block.tensor
        def _(pe):
            for n in range(G_BANKS):
                mt, half = n // 2, n % 2
                wait_count(pe, g_in, n - 3)
                for t in range(TPH):
                    last = pe.transpose(banks[n % 4][:, at(0, t, P)], k["graph"][:, half * TPH + t, at(0, mt, P)],
                                        k["ident"][:, :])
                last.then_inc(g_turned, 1)
            pe.wait_ge(g_in, G_BANKS)
            for order, source in ((0, x_cur.rearrange("p t b c -> p t (b c)")), (1, t1)):
                for t in range(NT):
                    n = order * NT + t
                    wait_count(pe, t_in, n - 3 if t or not order else n)
                    for m in range(NT):
                        last = pe.matmul(banks[n % 4], graph_t[:, m, at(0, t, P)], source[:, m, :],
                                         start=m == 0, stop=m == NT - 1)
                    last.then_inc(t_mm, 1)
            pe.wait_ge(t_in, 2 * NT)
            pe.wait_ge(w_in, 80)

            def tile(t, half):
                for g in range(PAIRS):
                    n = t * PAIRS + g
                    if g == 0:
                        pe.wait_ge(join_in, t + 1)
                    wait_count(pe, join_t_in, n - 1)
                    for j in range(4):
                        last = pe.transpose(banks[n % 2 if isinstance(n, int) else g % 2][:, at(0, j, P)],
                                            joined[half][:, 2 * g + j // 2, 2 * (j % 2):2 * (j % 2) + 2, :]
                                            .rearrange("p a c -> p (a c)"), k["ident"][:, :])
                    last.then_inc(join_mm, 1)
                    pe.wait_ge(join_t_in, n + 1)
                    for q in range(2):
                        m = 2 * n + q
                        wait_count(pe, prod_in, m - 1)
                        for part, w in ((0, w01), (1, w2b)):
                            for h in range(2):
                                last = pe.matmul(y[:, q, at(0, h, HALF)], joined_t[g % 2][:, 2 * q + part, :],
                                                 w[:, 8 * h:8 * h + 8, :].rearrange("p d c -> p (d c)"),
                                                 start=part == 0, stop=part == 1)
                        last.then_inc(y_mm, 1)
            tile(0, 0)
            with pe.Fori(1, NT - 2, 2) as t:
                tile(t, 1)
                tile(t + 1, 0)
            tile(NT - 1, 1)

        @block.scalar
        def _(act):
            for n in range(G_BANKS):
                act.wait_ge(g_turned, n + 1)
                act.activation(graph_t[:, n // 2, at(0, n % 2, HALF)], banks[n % 4], ACT.Copy).then_inc(g_in, 1)

            def tile(t):
                for g in range(PAIRS):
                    n = t * PAIRS + g
                    act.wait_ge(join_mm, n + 1)
                    wait_count(act, y_mm, 2 * n - 2)
                    act.activation(joined_t[g % 2][:, :, :], banks[g % 2].rearrange("p (j n) -> p j n", j=4),
                                   ACT.Copy).then_inc(join_t_in, 1)
            tile(0)
            with act.Fori(1, NT) as t:
                tile(t)

        @block.gpsimd
        def _(pool):
            pool.memset(w2b[:, :, :], 0.0).then_inc(cleared, 1)
            for half in range(2):
                pool.memset(joined[half][:, :, 3, 1:C], 0.0)
                pool.memset(joined[half][:, :, 3, 0:1], 1.0)
            pool.wait_ge(t_in, 2 * NT)

            def tile(t, half):
                wait_apart(pool, y_mm, (t - 1) * B, pool_passed)
                for order, source in enumerate((x_cur.rearrange("p t b c -> p t (b c)"), t1, t2)):
                    last = pool.tensor_copy(joined[half][:, :, order, :],
                                              (source[:, t, :] if isinstance(t, int) else
                                               source[:, bass.ds(t, 1), :].rearrange("p a n -> p (a n)"))
                                              .rearrange("p (b c) -> p b c", b=B))
                last.then_inc(join_in, 1)
            tile(0, 0)
            tile(1, 1)
            with pool.Fori(2, NT - 1, 2) as t:
                tile(t, 0)
                tile(t + 1, 1)

        @block.vector
        def _(dve):
            for n in range(2 * NT):
                t = n % NT
                dve.wait_ge(t_mm, n + 1)
                if n < NT:
                    dve.tensor_copy(t1[:, t, :], banks[n % 4]).then_inc(t_in, 1)
                else:
                    dve.scalar_tensor_tensor(out=t2[:, t, :], in0=banks[n % 4], scalar=2.0,
                                             in1=x_cur[:, t].rearrange("p b c -> p (b c)"),
                                             op0=ALU.mult, op1=ALU.subtract).then_inc(t_in, 1)
            dve.wait_ge(w_in, 80)

            def product(t, b):
                n = t * B + b
                dve.wait_ge(y_mm, n + 1)
                wait_count(dve, sum_in, n - 1)
                factors = emb[:, t, :] if isinstance(t, int) else emb[:, bass.ds(t, 1), :].rearrange("p a d -> p (a d)")
                dve.tensor_tensor(prods[:, b % 2], y[:, b % 2].rearrange("p (d c) -> p d c", c=C),
                                  factors.unsqueeze(2).broadcast_to([P, EMB, C]), ALU.mult).then_inc(prod_in, 1)

            def total(t, b):
                n = t * B + b
                dve.wait_ge(prod_in, n + 1)
                out = res[:, t, b, :] if isinstance(t, int) else \
                    res[:, bass.ds(t, 1), b, :].rearrange("p a c -> p (a c)")
                dve.tensor_reduce(out, prods[:, b % 2].rearrange("p d c -> p c d"), AX.X, ALU.add).then_inc(sum_in, 1)

            def tile(t, before):
                for b in range(B):
                    product(t, b)
                    if b:
                        total(t, b - 1)
                    elif before is not None:
                        total(before, B - 1)
            tile(0, None)
            with dve.Fori(1, NT) as t:
                tile(t, t - 1)
            total(NT - 1, B - 1)


def message_passing(nc, k, x_cur, res, graph_t, value, W1, b1, W2, b2):
    with ExitStack() as local:
        def sb(name, shape, dt=F32):
            return local.enter_context(nc.sbuf_tensor(name, shape, dt))

        def sem(name):
            return local.enter_context(nc.semaphore(name))

        v = sb("v", [P, NT, B * C])
        v_t = sb("v_t", [P, PAIRS, N])
        effect = [sb(f"effect{i}", [P, HALF]) for i in range(2)]
        hidden = [sb(f"hidden{i}", [P, HALF]) for i in range(2)]
        wn = sb("wn", [P, 3, P])
        wtr = sb("wtr", [P, 3, P])
        b1c, b2c = sb("b1c", [P, 1]), sb("b2c", [P, 1])
        b2r = sb("b2r", [P, C])
        banks = [local.enter_context(nc.psum_tensor(f"pm{i}", [P, HALF], F32))[:, :] for i in range(8)]
        e_bank, h_bank, n_bank, t_bank = banks[0:2], banks[2:4], banks[4:6], banks[6:8]
        cleared, w_in, v_in, v_set = sem("cleared3"), sem("w_in3"), sem("v_in3"), sem("v_set")
        turned, taken = sem("turned3"), sem("taken3")
        e_mm, e_in, h_mm, h_in = sem("e_mm"), sem("e_in"), sem("h_mm3"), sem("h_in3")
        n_mm, n_in, t_mm, t_in = sem("n_mm"), sem("n_in"), sem("t_mm3"), sem("t_in3")
        block = local.enter_context(nc.Block())
        SETUP = 1 + 2 * PAIRS
        KINDS = 2 * PAIRS

        @block.sync
        def _(sync):
            sync.wait_ge(cleared, 1)
            for q in range(2):
                d = slice(q * C, (q + 1) * C)
                for j, source in enumerate((W1[:, 0:C], W1[:, C:2 * C], W2)):
                    sync.dma_start(wn[d, j, d], source).then_inc(w_in, 16)
                sync.dma_start(b1c[d, :], b1.unsqueeze(1)).then_inc(w_in, 16)
                sync.dma_start(b2c[d, :], b2.unsqueeze(1)).then_inc(w_in, 16)
            sync.dma_start(b2r[:, :], b2.unsqueeze(0).broadcast_to([P, C])).then_inc(w_in, 16)
            sync.wait_ge(v_in, 1)
            sync.dma_start(v[0:1, 0, :].rearrange("p (b c) -> p b c", b=B),
                           value.unsqueeze(1).broadcast_to([1, B, C])).then_inc(v_set, 16)

        @block.gpsimd
        def _(pool):
            pool.memset(wn[:, :, :], 0.0).then_inc(cleared, 1)

        @block.tensor
        def _(pe):
            pe.wait_ge(w_in, 16 * 11)
            for j in range(3):
                last = pe.transpose(n_bank[0][:, at(0, j, P)], wn[:, j, :], k["ident"][:, :])
            last.then_inc(turned, 1)
            pe.wait_ge(v_set, 16)
            for g in range(2 * PAIRS):
                wait_count(pe, taken, g)
                for t in range(TPH):
                    last = pe.transpose(n_bank[(g + 1) % 2][:, at(0, t, P)],
                                        v[:, (g % 2) * TPH + t, at(0, g // 2, P)], k["ident"][:, :])
                last.then_inc(turned, 1)
            pe.wait_ge(taken, SETUP)

            def effects(r, g):
                pair, half = g // 2, g % 2
                n = r * KINDS + g
                if half == 0:
                    wait_count(pe, n_in, (r - 1) * KINDS + 2 * pair + 2)
                wait_count(pe, e_in, n - 1)
                for m in range(NT):
                    last = pe.matmul(e_bank[half], v[:, m, at(0, pair, P)], graph_t[:, m, at(0, half, HALF)],
                                     start=m == 0, stop=m == NT - 1)
                last.then_inc(e_mm, 1)

            def hiddens(r, g):
                pair, half = g // 2, g % 2
                n = r * KINDS + g
                wait_count(pe, t_in, (r - 1) * KINDS + g + 1)
                pe.wait_ge(e_in, n + 1)
                wait_count(pe, h_in, n - 1)
                pe.matmul(h_bank[half], wtr[:, 0, :], v_t[:, pair, at(0, half, HALF)], start=True, stop=False)
                pe.matmul(h_bank[half], wtr[:, 1, :], effect[half][:, :], start=False, stop=True).then_inc(h_mm, 1)

            def news(r, g):
                half = g % 2
                n = r * KINDS + g
                pe.wait_ge(h_in, n + 1)
                wait_count(pe, n_in, n - 1)
                for t in range(TPH):
                    last = pe.matmul(n_bank[half][:, at(0, t, P)], hidden[half][:, at(0, t, P)], wtr[:, 2, :],
                                     start=True, stop=True)
                last.then_inc(n_mm, 1)
                wait_count(pe, t_in, n - 1)
                pe.matmul(t_bank[half], wtr[:, 2, :], hidden[half][:, :], start=True, stop=True).then_inc(t_mm, 1)

            def step(r):
                for g in range(KINDS + 2):
                    if g < KINDS:
                        effects(r, g)
                    if 1 <= g <= KINDS:
                        hiddens(r, g - 1)
                    if g >= 2:
                        news(r, g - 2)
            step(0)
            with pe.Fori(1, STEPS) as r:
                step(r)

        @block.vector
        def _(dve):
            dve.tensor_copy(v[:, :, :], x_cur.rearrange("p t b c -> p t (b c)")).then_inc(v_in, 1)
            for g in range(SETUP):
                dve.wait_ge(turned, g + 1)
                if g == 0:
                    dve.tensor_copy(wtr[:, :, :], n_bank[0][:, 0:3 * P].rearrange("p (j n) -> p j n", j=3)).then_inc(taken, 1)
                else:
                    q = g - 1
                    dve.tensor_copy(v_t[:, q // 2, at(0, q % 2, HALF)], n_bank[g % 2]).then_inc(taken, 1)

            def step(r):
                for g in range(KINDS):
                    pair, half = g // 2, g % 2
                    n = r * KINDS + g
                    dve.wait_ge(n_mm, n + 1)
                    if half == 0:
                        dve.wait_ge(e_mm, n + 2)
                    dve.tensor_tensor(v[:, half * TPH:(half + 1) * TPH, at(0, pair, P)]
                                      .rearrange("p t (b c) -> p t b c", b=2),
                                      n_bank[half].rearrange("p (t b c) -> p t b c", t=TPH, b=2),
                                      b2r[:, :].unsqueeze(1).unsqueeze(1).broadcast_to([P, TPH, 2, C]),
                                      ALU.add).then_inc(n_in, 1)
            step(0)
            with dve.Fori(1, STEPS) as r:
                step(r)
            dve.wait_ge(n_in, STEPS * KINDS)
            dve.tensor_copy(res.rearrange("p t b c -> p t (b c)"), v[:, :, :])

        @block.scalar
        def _(act):
            act.wait_ge(w_in, 16 * 11)

            def step(r):
                for g in range(KINDS + 2):
                    if g < KINDS:
                        half, n = g % 2, r * KINDS + g
                        act.wait_ge(e_mm, n + 1)
                        wait_count(act, h_mm, n - 1)
                        act.activation(effect[half][:, :], e_bank[half], ACT.Copy).then_inc(e_in, 1)
                    if 1 <= g <= KINDS:
                        half, n = (g - 1) % 2, r * KINDS + g - 1
                        act.wait_ge(h_mm, n + 1)
                        wait_count(act, t_mm, n - 1)
                        act.activation(hidden[half][:, :], h_bank[half], ACT.Relu, bias=b1c[:, 0:1]).then_inc(h_in, 1)
                    if g >= 2:
                        pair, half, n = (g - 2) // 2, g % 2, r * KINDS + g - 2
                        act.wait_ge(t_mm, n + 1)
                        act.activation(v_t[:, pair, at(0, half, HALF)], t_bank[half], ACT.Identity,
                                       bias=b2c[:, 0:1]).then_inc(t_in, 1)
            step(0)
            with act.Fori(1, STEPS) as r:
                step(r)


def graph_stack(nc, x, adj, L0_gnn_Wh, L0_gnn_bh, L0_gnn_W_out, L0_gnn_b_out, L1_gnn_embedding, L1_gnn_weight,
                L1_gnn_bias, L2_gnn_intervention_value, L2_gnn_W1, L2_gnn_b1, L2_gnn_W2, L2_gnn_b2, L3_gnn_W,
                L3_gnn_a, out):
    with ExitStack() as ctx:
        k = constants(nc, ctx, adj)
        res = ctx.enter_context(nc.sbuf_tensor("res", [P, NT, B, C], F32))[:, :, :, :]
        xv = x.rearrange("b (t p) c -> p t b c", p=P)

        sums = res.rearrange("p t b c -> p t (b c)")
        with ExitStack() as layer:
            def sb(name, shape, dt=F32):
                return layer.enter_context(nc.sbuf_tensor(name, shape, dt))
            xs = sb("xs", [P, B, N], F32R)
            gram, head_w = sb("head_gram", [P, HEADS, 2, P], F32R), sb("head_w", [P, HEADS, HID])
            out_w, head_b = sb("out_w", [P, HEADS, C]), sb("head_b", [P, HEADS, 2])
            prepare_heads(nc, k, x, L0_gnn_Wh, L0_gnn_bh, L0_gnn_W_out, xs, gram, head_w, out_w, head_b, sums)

            def x_of(b):
                if isinstance(b, int):
                    return x[b].rearrange("(t p) c -> p t c", p=P)
                return x[bass.ds(b, 1)].rearrange("a (t p) c -> p (a t) c", p=P)
            attention(nc, k, HEAD_UNITS, x_of, sums, xs, gram, head_w, out_w, head_b)

        def values_of(tensor):
            def of(b):
                if isinstance(b, int):
                    return tensor[:, :, b, :]
                return tensor[:, :, bass.ds(b, 1), :].rearrange("p t a c -> p t (a c)")
            return of

        with ExitStack() as layer:
            xs = layer.enter_context(nc.sbuf_tensor("xs2", [P, B, N], F32R))
            nat = layer.enter_context(nc.sbuf_tensor("nat2", [P, NT, B, C], F32))
            prepare_output_head(nc, k, sums, xs, nat)
            attention(nc, k, OUTPUT_UNITS, values_of(nat), res, xs)

        x_cur_t = ctx.enter_context(nc.sbuf_tensor("x_cur", [P, NT, B, C], F32))
        x_cur = x_cur_t[:, :, :, :]
        layer_norm(nc, "norm1", x_cur, res, ("leaky", L0_gnn_b_out.unsqueeze(0).broadcast_to([P, C])),
                   [(x_cur[:, t], xv[:, t]) for t in range(NT)])

        with ExitStack() as layer:
            graph_t = layer.enter_context(nc.sbuf_tensor("graph_t", [P, NT, N], F32))
            chebyshev(nc, k, x_cur, res, graph_t, L1_gnn_embedding, L1_gnn_weight, L1_gnn_bias)
            layer_norm(nc, "norm2", x_cur, res, ("none",))
            message_passing(nc, k, x_cur, res, graph_t, L2_gnn_intervention_value, L2_gnn_W1, L2_gnn_b1,
                            L2_gnn_W2, L2_gnn_b2)
            layer_norm(nc, "norm3", x_cur, res, ("none",))

        with ExitStack() as layer:
            def sb(name, shape, dt=F32):
                return layer.enter_context(nc.sbuf_tensor(name, shape, dt))
            nat = sb("nat4", [P, NT, B, C])
            src_score, dst_w, x_pairs = sb("src_score", [P, B, NT]), sb("dst_w", [P, 2, P]), sb("x_pairs4", [P, PAIRS, N])
            prepare_edges(nc, k, x_cur.rearrange("p t b c -> p t (b c)"), L3_gnn_W, L3_gnn_a, nat, src_score, dst_w, x_pairs)
            attention(nc, k, EDGE_UNITS, values_of(nat), res, src_score=src_score, dst_w=dst_w, x_pairs=x_pairs)
        layer_norm(nc, "norm4", x_cur, res, ("elu",))

        with ExitStack() as local:
            stored = local.enter_context(nc.semaphore("stored"))
            block = local.enter_context(nc.Block())
            ov = out.rearrange("b (t p) c -> p t b c", p=P)

            @block.sync
            def _(sync):
                for t in range(NT):
                    sync.dma_start(ov[:, t], x_cur[:, t]).then_inc(stored, 16)
                sync.wait_ge(stored, 16 * NT)


_INS = ['x', 'adj', 'L0_gnn_Wh', 'L0_gnn_bh', 'L0_gnn_W_out', 'L0_gnn_b_out', 'L1_gnn_embedding', 'L1_gnn_weight',
        'L1_gnn_bias', 'L2_gnn_intervention_value', 'L2_gnn_W1', 'L2_gnn_b1', 'L2_gnn_W2', 'L2_gnn_b2', 'L3_gnn_W',
        'L3_gnn_a']


def kernel(**inputs):
    import numpy as np
    import concourse.bacc as bacc
    from concourse import mybir as _mybir
    from concourse.bass_utils import run_bass_kernel_spmd

    nc = bacc.Bacc("TRN2", target_bir_lowering=False, num_devices=1)
    arrays, args = {}, []
    for name in _INS:
        a = np.ascontiguousarray(inputs[name])
        arrays[f"in_{name}"] = a
        args.append(nc.dram_tensor(f"in_{name}", a.shape, _mybir.dt.from_np(a.dtype), kind="ExternalInput").ap())
    out = nc.dram_tensor("out_0", (B, N, C), F32, kind="ExternalOutput").ap()
    graph_stack(nc, *args, out)
    r = run_bass_kernel_spmd(nc, [arrays], core_ids=[0])
    return r.results[0]["out_0"]
```

```python
from contextlib import ExitStack

import concourse.bass as bass
from concourse import mybir

F32 = mybir.dt.float32
F32R = mybir.dt.float32r
ALU = mybir.AluOpType
ACT = mybir.ActivationFunctionType
AX = mybir.AxisListType

P = 128
B = 8
N = 1024
C = 64
HEADS = 8
HID = 128
NT = N // P
HALF = N // 2
PAIRS = B // 2
TPH = NT // 2
EMB = 16
ORDERS = 3
STEPS = 3
LEAK_HEADS = 0.01
NEG_HEADS = -1e16
NEG_EDGES = -9000000000000000.0
BIG = 3.0e38
EPS = 1e-5


def wait_count(engine, sem, value):
    if isinstance(value, int) and value <= 0:
        return
    engine.wait_ge(sem, value)


def wait_apart(engine, sem, value, passed):
    if isinstance(value, int):
        wait_count(engine, sem, value)
    else:
        engine.wait_ge(sem, value)
        engine.sem_inc(passed, 1)


def at(base, index, size):
    if isinstance(index, int):
        return slice(base + index * size, base + (index + 1) * size)
    return bass.ds(index * size + base, size)


def constants(nc, ctx, adj):
    def sb(name, shape, dt=F32):
        return ctx.enter_context(nc.sbuf_tensor(name, shape, dt))

    k = {
        "ident": sb("ident", [P, P]),
        "dup0": sb("dup0", [P, P]),
        "dup1": sb("dup1", [P, P]),
        "dups": sb("dups", [P, P]),
        "dups_r": sb("dups_r", [P, P], F32R),
        "graph": sb("graph", [P, NT, N]),
    }
    with ExitStack() as local:
        def sem(name):
            return local.enter_context(nc.semaphore(name))
        cleared, ident_made, dup_made, graph_in = sem("cleared"), sem("ident_made"), sem("dup_made"), sem("graph_in")
        block = local.enter_context(nc.Block())

        @block.sync
        def _(sync):
            sync.dma_start(k["graph"][:, :, :], adj.rearrange("(t p) m -> p t m", p=P)).then_inc(graph_in, 16)
            sync.wait_ge(graph_in, 16)

        @block.gpsimd
        def _(pool):
            pool.memset(k["ident"][:, :], 0.0).then_inc(cleared, 1)
            pool.wait_ge(cleared, 1)
            pool.affine_select(out=k["ident"][:, :], in_=k["ident"][:, :], compare_op=ALU.not_equal, fill=1.0,
                               base=0, pattern=[[-1, P]], channel_multiplier=1).then_inc(ident_made, 1)

        @block.vector
        def _(dve):
            dve.wait_ge(ident_made, 1)
            for col in (0, C):
                dve.tensor_copy(k["dup0"][:, col:col + C], k["ident"][:, 0:C]).then_inc(dup_made, 1)
                dve.tensor_copy(k["dup1"][:, col:col + C], k["ident"][:, C:P]).then_inc(dup_made, 1)
            dve.wait_ge(dup_made, 4)
            for dups in ("dups", "dups_r"):
                dve.tensor_tensor(k[dups][:, :], k["dup0"][:, :], k["dup1"][:, :], ALU.add)
    return k


def stack_parts(block, k, source, stacked, banks, ready, stacked_mm, high_in, low_in):
    slots = len(banks)

    @block.tensor
    def _(pe):
        ready(pe)
        for n in range(2 * B):
            moving, copies = source(n // 2, n % 2)
            wait_count(pe, low_in, n - slots + 1)
            pe.matmul(banks[n % slots], copies, moving, start=True, stop=True).then_inc(stacked_mm, 1)

    @block.scalar
    def _(act):
        for n in range(2 * B):
            act.wait_ge(stacked_mm, n + 1)
            act.activation(stacked[:, n // 2, at(0, n % 2, HALF)], banks[n % slots], ACT.Copy).then_inc(high_in, 1)

    @block.vector
    def _(dve):
        for n in range(2 * B):
            low = stacked[C:P, n // 2, at(0, n % 2, HALF)]
            dve.wait_ge(high_in, n + 1)
            dve.tensor_tensor(low, banks[n % slots][C:P, :], low.bitcast(F32), ALU.subtract).then_inc(low_in, 1)


def prepare_heads(nc, k, x, Wh, bh, W_out, xs, head_gram, head_w, out_w, head_b, sums):
    with ExitStack() as local:
        def sb(name, shape, dt=F32):
            return local.enter_context(nc.sbuf_tensor(name, shape, dt))

        def sem(name):
            return local.enter_context(nc.semaphore(name))

        x_nat = sb("x_nat", [P, NT, B * C])
        x_pairs = sb("x_pairs", [P, PAIRS, N])
        wt = sb("wt", [P, HEADS, P])
        banks = [local.enter_context(nc.psum_tensor(f"ph{i}", [P, HALF], F32))[:, :] for i in range(8)]
        w_in, x_in, turned, taken = sem("w_in"), sem("x_in"), sem("turned"), sem("taken")
        stacked_mm, high_in, low_in = sem("stacked_mm"), sem("high_in"), sem("low_in")
        block = local.enter_context(nc.Block())
        W_BANKS = HEADS // 4

        @block.sync
        def _(sync):
            for copy in (0, C):
                sync.dma_start(head_w[copy:copy + C, :, :], Wh.rearrange("h c d -> c h d")).then_inc(w_in, 16)
            sync.dma_start(out_w[:, :, :], W_out.rearrange("(h d) o -> d h o", d=HID)).then_inc(w_in, 16)
            sync.dma_start(head_b[:, :, 0], bh.rearrange("h d -> d h"), allow_slow_non_contiguous=True).then_inc(w_in, 16)
            xv = x.rearrange("b (t p) c -> p t b c", p=P)
            for t in range(NT):
                sync.dma_start(x_nat[:, t, :].rearrange("p (b c) -> p b c", b=B), xv[:, t]).then_inc(x_in, 16)

        @block.gpsimd
        def _(pool):
            pool.memset(sums[:, :, :], 0.0)

        @block.tensor
        def _(pe):
            pe.wait_ge(w_in, 64)
            for h in range(HEADS):
                last = pe.transpose(banks[h // 4][:, at(0, h % 4, P)], head_w[:, h, :], k["ident"][:, :])
                if h % 4 == 3:
                    last.then_inc(turned, 1)
            pe.wait_ge(x_in, 16 * NT)
            for g in range(PAIRS * 2):
                bank = banks[(W_BANKS + g) % 8]
                wait_count(pe, taken, W_BANKS + g - 7)
                for t in range(TPH):
                    last = pe.transpose(bank[:, at(0, t, P)], x_nat[:, (g % 2) * TPH + t, at(0, g // 2, P)],
                                        k["ident"][:, :])
                last.then_inc(turned, 1)
            pe.wait_ge(taken, W_BANKS + 2 * PAIRS)
            for h in range(HEADS):
                last = pe.matmul(banks[h // 4][:, at(0, h % 4, P)], wt[:, h, :], wt[:, h, :], start=True, stop=True)
                if h % 4 == 3:
                    last.then_inc(turned, 1)

        @block.vector
        def _(dve):
            dve.wait_ge(w_in, 64)
            dve.tensor_scalar(head_b[:, :, 1], head_b[:, :, 0], -LEAK_HEADS, None, ALU.mult)
            for g in range(W_BANKS + 2 * PAIRS):
                dve.wait_ge(turned, g + 1)
                if g < W_BANKS:
                    out = wt[:, 4 * g:4 * g + 4, :]
                    dve.tensor_copy(out, banks[g].rearrange("p (h d) -> p h d", h=4)).then_inc(taken, 1)
                else:
                    q = g - W_BANKS
                    dve.tensor_copy(x_pairs[:, q // 2, at(0, q % 2, HALF)], banks[g % 8]).then_inc(taken, 1)
            for g in range(W_BANKS):
                dve.wait_ge(turned, W_BANKS + 2 * PAIRS + g + 1)
                high, low = (head_gram[:, 4 * g:4 * g + 4, part, :] for part in range(2))
                gram = banks[g].rearrange("p (h d) -> p h d", h=4)
                dve.tensor_copy(high, gram).then_inc(taken, 1)
                dve.wait_ge(taken, W_BANKS + 2 * PAIRS + 2 * g + 1)
                dve.tensor_tensor(low, gram, high.bitcast(F32), ALU.subtract).then_inc(taken, 1)

        stack_parts(block, k,
                    lambda b, half: (x_pairs[:, b // 2, at(0, half, HALF)], k[f"dup{b % 2}"][:, :]),
                    xs, banks[4:8], lambda pe: pe.wait_ge(taken, 3 * W_BANKS + 2 * PAIRS),
                    stacked_mm, high_in, low_in)


def prepare_output_head(nc, k, sums, xs, nat):
    with ExitStack() as local:
        def sem(name):
            return local.enter_context(nc.semaphore(name))

        banks = [local.enter_context(nc.psum_tensor(f"po{i}", [P, HALF], F32))[:, :] for i in range(8)]
        turned, taken = sem("turned2"), sem("taken2")
        stacked_mm, high_in, low_in = sem("stacked_mm2"), sem("high_in2"), sem("low_in2")
        block = local.enter_context(nc.Block())

        @block.tensor
        def _(pe):
            for b in range(B):
                wait_count(pe, taken, b - 3)
                for t in range(TPH):
                    last = pe.transpose(banks[b % 4][:, at(0, t, P)], sums[:, b, at(0, t, P)], k["ident"][:, :])
                last.then_inc(turned, 1)

        @block.vector
        def _(dve):
            for b in range(B):
                dve.wait_ge(turned, b + 1)
                dve.tensor_copy(nat[:, :, b, :].rearrange("p (h t) c -> p t h c", h=2),
                                banks[b % 4].rearrange("p (t h c) -> p t h c", t=TPH, h=2)).then_inc(taken, 1)

        stack_parts(block, k, lambda b, half: (sums[:, b, :], k[f"dup{half}"][:, :]),
                    xs, banks[4:8], lambda pe: None, stacked_mm, high_in, low_in)


def prepare_edges(nc, k, x_cur, W, a, nat, src_score, dst_w, x_pairs):
    with ExitStack() as local:
        def sb(name, shape, dt=F32):
            return local.enter_context(nc.sbuf_tensor(name, shape, dt))

        def sem(name):
            return local.enter_context(nc.semaphore(name))

        WIDE = P + 2
        w2 = sb("w2", [P, WIDE])
        w2t = sb("w2t", [P, P])
        a4 = sb("a4", [P, 4])
        wa = sb("wa", [P, 4])
        ones = sb("ones", [P, P])
        banks = [local.enter_context(nc.psum_tensor(f"pe{i}", [P, HALF], F32))[:, :] for i in range(8)]
        cleared, w_in, turned, taken, made = sem("cleared4"), sem("w_in4"), sem("turned4"), sem("taken4"), sem("made4")
        h_mm, h_in, masked = sem("h_mm"), sem("h_in"), sem("masked4")
        block = local.enter_context(nc.Block())

        @block.sync
        def _(sync):
            sync.wait_ge(cleared, 2)
            for q in range(2):
                rows = slice(q * C, (q + 1) * C)
                sync.dma_start(w2[rows, q * C:(q + 1) * C], W).then_inc(w_in, 16)
                sync.dma_start(a4[rows, q:q + 1], a[0:C, :]).then_inc(w_in, 16)
                sync.dma_start(a4[rows, 2 + q:3 + q], a[C:2 * C, :]).then_inc(w_in, 16)

        @block.gpsimd
        def _(pool):
            pool.memset(w2[:, :], 0.0).then_inc(cleared, 1)
            pool.memset(a4[:, :], 0.0).then_inc(cleared, 1)
            pool.memset(ones[:, :], 1.0).then_inc(cleared, 1)

        @block.tensor
        def _(pe):
            pe.wait_ge(w_in, 96)
            pe.transpose(banks[0][:, 0:P], w2[:, 0:P], k["ident"][:, :]).then_inc(turned, 1)
            for g in range(2 * PAIRS):
                bank = banks[(1 + g) % 8]
                wait_count(pe, taken, g - 6)
                for t in range(TPH):
                    last = pe.transpose(bank[:, at(0, t, P)], x_cur[:, (g % 2) * TPH + t, at(0, g // 2, P)],
                                        k["ident"][:, :])
                last.then_inc(turned, 1)
            pe.wait_ge(taken, 1 + 2 * PAIRS)
            pe.matmul(banks[0][:, 0:4], w2t[:, :], a4[:, :], start=True, stop=True).then_inc(turned, 1)
            pe.wait_ge(made, 1)
            for n in range(PAIRS * NT):
                wait_count(pe, h_in, n - 3)
                pe.matmul(banks[1 + n % 4][:, 0:WIDE], x_pairs[:, n // NT, at(0, n % NT, P)], w2[:, :],
                          start=True, stop=True).then_inc(h_mm, 1)

        @block.vector
        def _(dve):
            dve.wait_ge(turned, 1)
            dve.tensor_copy(w2t[:, :], banks[0][:, 0:P]).then_inc(taken, 1)
            for g in range(2 * PAIRS):
                dve.wait_ge(turned, g + 2)
                dve.tensor_copy(x_pairs[:, g // 2, at(0, g % 2, HALF)], banks[(1 + g) % 8]).then_inc(taken, 1)
            dve.wait_ge(turned, 2 + 2 * PAIRS)
            dve.tensor_copy(wa[:, :], banks[0][:, 0:4]).then_inc(taken, 1)
            dve.wait_ge(taken, 2 + 2 * PAIRS)
            dve.tensor_copy(w2[:, P:WIDE], wa[:, 0:2]).then_inc(made, 1)
            dve.wait_ge(cleared, 3)
            for q in range(2):
                dve.tensor_scalar(dst_w[:, q, :], ones[:, :], wa[:, 2 + q:3 + q], None, ALU.mult)
            for t in range(NT):
                dve.tensor_scalar(k["graph"][:, t, :], k["graph"][:, t, :], 0.5, NEG_EDGES, ALU.is_le, ALU.mult)

        @block.scalar
        def _(act):
            for n in range(PAIRS * NT):
                pair, t = n // NT, n % NT
                bank = banks[1 + n % 4]
                act.wait_ge(h_mm, n + 1)
                act.activation(nat[:, t, 2 * pair:2 * pair + 2, :],
                               bank[:, 0:P].rearrange("p (b c) -> p b c", b=2), ACT.Copy)
                act.activation(src_score[:, 2 * pair:2 * pair + 2, t], bank[:, P:WIDE], ACT.Copy).then_inc(h_in, 1)


QUERY_TURN = 4
HEAD_UNITS, OUTPUT_UNITS, EDGE_UNITS = "heads", "output", "edges"
LAG_EXP, LAG_RECIP, LAG_TURN = 1, 2, 3
HALF0_TILES = {0: (0, 4), 1: (4, 6), 2: (6, 8)}
HALF1_TILES = {4: (0, 4), 5: (4, 6), 6: (6, 8)}
AFTER0, AFTER1 = 3, 7


def attention(nc, k, kind, values, res, xs=None, head_gram=None, head_w=None, out_w=None, head_b=None,
              src_score=None, dst_w=None, x_pairs=None):
    units = B * HEADS if kind == HEAD_UNITS else B
    split = kind != EDGE_UNITS

    def batch(U):
        return U // HEADS if kind == HEAD_UNITS else U

    with ExitStack() as local:
        def sb(name, shape, dt=F32):
            return local.enter_context(nc.sbuf_tensor(f"{kind}_{name}", shape, dt))

        def psum(name, shape):
            return local.enter_context(nc.psum_tensor(f"{kind}_{name}", shape, F32))

        def sem(name):
            return local.enter_context(nc.semaphore(f"{kind}_{name}"))

        S = psum("S", [P, 2, N])
        turn = psum("turn", [P, 2, HALF])
        mix = psum("mix", [P, HALF])
        back = psum("back", [P, HALF])

        prod = sb("prod", [P, 2, N])
        floor = sb("floor", [P, 2, N], mybir.dt.bfloat16 if split else F32)
        neg = sb("neg", [P, 2, N])
        e = sb("e", [P, 4, N])
        neg_max = sb("neg_max", [P, 2, NT])
        row_sum = sb("row_sum", [P, 2, NT])
        row_inv = sb("row_inv", [P, 2, NT])
        weights_t = sb("weights_t", [P, 2, NT, HALF])
        val = [sb(f"val{i}", [P, NT, C]) for i in range(2)]
        mixed = [sb(f"mixed{i}", [P, HALF]) for i in range(2)]
        if split:
            q_high = [sb(f"q_high{i}", [P, N], F32R) for i in range(2)]
            q_low = [sb(f"q_low{i}", [P, N], F32R) for i in range(2)]
        else:
            dst = sb("dst", [P, 2, N])
            src = sb("src", [P, 2, NT])
        if kind == HEAD_UNITS:
            gram = [sb(f"gram{i}", [P, 2, P], F32R) for i in range(2)]
            w_now = [sb(f"w_now{i}", [P, HID]) for i in range(2)]
            ow_now = [sb(f"ow_now{i}", [P, C]) for i in range(2)]
            b_now = [sb(f"b_now{i}", [P, 2]) for i in range(2)]
            above = [sb(f"above{i}", [P, HALF]) for i in range(2)]
            below = [sb(f"below{i}", [P, HALF]) for i in range(2)]
            cat = [sb(f"cat{i}", [P, HALF]) for i in range(2)]

        val_in = [sem(f"val_in{i}") for i in range(2)]
        if split:
            q_mm, q_high_in, q_low_in, scored = sem("q_mm"), sem("q_high_in"), sem("q_low_in"), sem("scored")
        else:
            dst_mm, dst_in, src_in = sem("dst_mm"), sem("dst_in"), sem("src_in")
        if kind == HEAD_UNITS:
            gram_in, back_in = sem("gram_in"), sem("back_in")
            head_mm, biased, cat_in = sem("head_mm"), sem("biased"), sem("cat_in")
        prod_in, floor_in, max_in = sem("prod_in"), sem("floor_in"), sem("max_in")
        exp_in, inv_in, normed = sem("exp_in"), sem("inv_in"), sem("normed")
        turned, turned_in = sem("turned"), sem("turned_in")
        mixed_mm, mixed_in = sem("mixed_mm"), sem("mixed_in")
        out_mm, out_in = sem("out_mm"), sem("out_in")
        dve_passed, pool_passed = sem("dve_passed"), sem("pool_passed")
        block = local.enter_context(nc.Block())

        def run(engine, unit, tail):
            unit(0, 0, None, None)
            unit(1, 1, 0, None)
            with engine.Fori(2, units - 3, 2) as U:
                unit(U, 0, U - 1, U - 2)
                unit(U + 1, 1, U, U - 1)
            unit(units - 2, 0, units - 3, units - 4)
            unit(units - 1, 1, units - 2, units - 3)
            tail(units - 1, units - 2)

        def lagged(U, V, s, lag):
            return (U, True, s - lag) if s >= lag else (V, False, s - lag + NT)

        def slot_of(u, i):
            return (u + i + (i >= QUERY_TURN)) % 2

        def query_slot(w):
            return (1 - w + QUERY_TURN) % 2

        @block.tensor
        def _(pe):
            def queries(W, w):
                if not split:
                    return
                slot = S[:, query_slot(w), :]
                if kind == HEAD_UNITS:
                    pe.wait_ge(gram_in, W + 1)
                wait_count(pe, prod_in, (W - 1) * NT + QUERY_TURN - 1)
                parts = [gram[w][:, part, :] for part in range(2)] if kind == HEAD_UNITS else [k["dups_r"][:, :]]
                for n, part in enumerate(parts):
                    for half in range(2):
                        last = pe.matmul(slot[:, at(0, half, HALF)], part, xs[:, batch(W), at(0, half, HALF)],
                                         start=n == 0, stop=n == len(parts) - 1)
                last.then_inc(q_mm, 1)

            def destinations(W, w, q):
                wait_count(pe, dst_in, W - 1)
                for half in range(2):
                    last = pe.matmul(S[:, w, at(0, half, HALF)], dst_w[:, q, :],
                                     x_pairs[:, W // 2, at(0, half, HALF)], start=True, stop=True)
                last.then_inc(dst_mm, 1)

            def scores(U, u, i):
                if not split:
                    return
                if i == 0:
                    pe.wait_ge(q_low_in, U + 1)
                if i == QUERY_TURN + 1 and not (isinstance(U, int) and U == units - 1):
                    pe.wait_ge(q_low_in, U + 2)
                wait_count(pe, prod_in, U * NT + (i if i == QUERY_TURN else i - 1))
                for n, part in enumerate((q_high, q_low)):
                    for half in range(2):
                        last = pe.matmul(S[:, slot_of(u, i), at(0, half, HALF)], part[u][:, at(0, i, P)],
                                         xs[:, batch(U), at(0, half, HALF)], start=n == 0, stop=n == 1)
                last.then_inc(scored, 1)

            def transposes(V, i):
                T = V * NT + i
                pe.wait_ge(normed, T + 1)
                for g in range(2):
                    wait_count(pe, turned_in, 2 * T + g - 1)
                    for j in range(TPH):
                        last = pe.transpose(turn[:, g, at(0, j, P)], e[:, i % 4, at(0, g * TPH + j, P)],
                                            k["ident"][:, :])
                    last.then_inc(turned, 1)

            def mixing(V, v, half, first, end):
                if first == 0:
                    pe.wait_ge(turned_in, 2 * (V * NT + (half + 1) * TPH))
                    if half == 0:
                        pe.wait_ge(val_in[v], 16 * (V // 2 + 1))
                for t in range(first, end):
                    rows = slice(C * (t % 2), C * (t % 2) + C)
                    last = pe.matmul(mix[rows, :], val[v][:, t, :], weights_t[:, half, t, :],
                                     start=t < 2, stop=t >= NT - 2)
                if end == NT:
                    last.then_inc(mixed_mm, 1)

            def after(V, v, half):
                n = 2 * V + half
                pe.wait_ge(mixed_in, n + 1)
                if kind == HEAD_UNITS:
                    if half == 0:
                        pe.wait_ge(back_in, V + 1)
                        pe.wait_ge(out_in, V + 1)
                    else:
                        pe.wait_ge(biased, n)
                    pe.matmul(back[:, :], w_now[v][:, :], mixed[half][:, :], start=True, stop=True).then_inc(head_mm, 1)
                else:
                    for t in range(TPH):
                        last = pe.matmul(back[:, at(0, t, C)], mixed[half][:, at(0, t, P)], k["dups"][:, 0:C],
                                         start=True, stop=True)
                    last.then_inc(out_mm, 1)

            def outputs(V, v):
                if kind != HEAD_UNITS:
                    return
                pe.wait_ge(cat_in, 2 * V + 2)
                for half in range(2):
                    last = pe.matmul(back[half * C:half * C + C, :], ow_now[v][:, :], cat[half][:, :],
                                     start=True, stop=True)
                last.then_inc(out_mm, 1)

            def behind(V, v, s):
                if s in HALF0_TILES:
                    mixing(V, v, 0, *HALF0_TILES[s])
                if s in HALF1_TILES:
                    mixing(V, v, 1, *HALF1_TILES[s])

            def behind_turned(V, v, s):
                if s == AFTER0:
                    after(V, v, 0)
                if s == AFTER1:
                    after(V, v, 1)

            def unit(U, u, V, V2):
                more = not (isinstance(U, int) and U == units - 1)
                for s in range(NT):
                    scores(U, u, s)
                    if s == QUERY_TURN - 1 and more:
                        queries(U + 1, 1 - u)
                    if V is not None:
                        behind(V, 1 - u, s)
                    if s == 2 and V2 is not None:
                        outputs(V2, u)
                    W, _, i = lagged(U, V, s, LAG_TURN)
                    if W is not None:
                        transposes(W, i)
                    if V is not None:
                        behind_turned(V, 1 - u, s)
                    if s == 2 and more and not split:
                        destinations(U + 1, 1 - u, 1 - u)

            queries(0, 0)
            if not split:
                destinations(0, 0, 0)

            def tail(V, V2):
                for s in range(NT):
                    if s == 2:
                        outputs(V2, 0)
                    behind(V, 1, s)
                    if s < LAG_TURN:
                        transposes(V, s - LAG_TURN + NT)
                    behind_turned(V, 1, s)
                outputs(V, 1)
            run(pe, unit, tail)

        @block.vector
        def _(dve):
            def masking(U, u, i):
                T = U * NT + i
                wait_count(dve, max_in, T - 1)
                if split:
                    dve.wait_ge(scored, T + 1)
                    dve.tensor_tensor(prod[:, i % 2, :], S[:, slot_of(u, i), :], k["graph"][:, i, :],
                                      ALU.mult).then_inc(prod_in, 1)
                else:
                    if i == 0:
                        dve.wait_ge(dst_in, U + 1)
                        dve.tensor_copy(src[:, u, :], src_score[:, batch(U), :] if isinstance(U, int) else
                                        src_score[:, bass.ds(U, 1), :].rearrange("p a t -> p (a t)")).then_inc(src_in, 1)
                        dve.wait_ge(src_in, U + 1)
                    dve.tensor_scalar(prod[:, i % 2, :], dst[:, u, :], src[:, u, i:i + 1], None,
                                      ALU.add).then_inc(prod_in, 1)

            def flooring(U, i):
                T = U * NT + i
                dve.wait_ge(prod_in, T + 1)
                wait_count(dve, max_in, T - 1)
                if split:
                    dve.tensor_scalar(floor[:, i % 2, :], prod[:, i % 2, :], 0.0, NEG_HEADS,
                                      ALU.is_equal, ALU.mult).then_inc(floor_in, 1)
                else:
                    dve.scalar_tensor_tensor(out=floor[:, i % 2, :], in0=prod[:, i % 2, :], scalar=0.2,
                                             in1=prod[:, i % 2, :], op0=ALU.mult, op1=ALU.max).then_inc(floor_in, 1)

            def maximum(V, v, i):
                T = V * NT + i
                wait_count(dve, floor_in, T + 1)
                wait_apart(dve, exp_in, T - 1, dve_passed)
                if split:
                    in0, in1 = prod[:, i % 2, :], floor[:, i % 2, :]
                else:
                    in0, in1 = floor[:, i % 2, :], k["graph"][:, i, :]
                dve.tensor_tensor_reduce(neg[:, i % 2, :], in0, in1, -1.0, BIG, ALU.add, ALU.min,
                                         neg_max[:, v, i:i + 1]).then_inc(max_in, 1)

            def inverse(V, v, i):
                dve.wait_ge(exp_in, V * NT + i + 1)
                dve.reciprocal(row_inv[:, v, i:i + 1], row_sum[:, v, i:i + 1]).then_inc(inv_in, 1)

            def low_part(W, w):
                if not split:
                    return
                dve.wait_ge(q_high_in, W + 1)
                dve.tensor_tensor(q_low[w][:, :], S[:, query_slot(w), :], q_high[w][:, :].bitcast(F32),
                                  ALU.subtract).then_inc(q_low_in, 1)

            def add_heads(V):
                if kind != HEAD_UNITS:
                    return
                dve.wait_ge(out_mm, V + 1)
                dve.wait_ge(out_in, V + 1)
                dve.tensor_tensor(res[:, batch(V), :], res[:, batch(V), :], back[:, :], ALU.add).then_inc(out_in, 1)

            def unit(U, u, V, V2):
                for s in range(NT):
                    masking(U, u, s)
                    W, same, i = lagged(U, V, s, LAG_RECIP)
                    if W is not None:
                        inverse(W, u if same else 1 - u, i)
                    if s == QUERY_TURN and not (isinstance(U, int) and U == units - 1):
                        low_part(U + 1, 1 - u)
                    W, same, i = lagged(U, V, s, LAG_EXP)
                    if W is not None:
                        maximum(W, u if same else 1 - u, i)
                    flooring(U, s)
                    if s == 2 and V2 is not None:
                        add_heads(V2)

            if kind == HEAD_UNITS:
                dve.memset(res[:, :, :], 0.0).then_inc(out_in, 1)
            low_part(0, 0)

            def tail(V, V2):
                for s in range(LAG_RECIP):
                    if s == 0:
                        maximum(V, 1, NT - 1)
                    inverse(V, 1, s - LAG_RECIP + NT)
                add_heads(V2)
                add_heads(V)
            run(dve, unit, tail)

        @block.scalar
        def _(act):
            def exponent(V, v, i):
                T = V * NT + i
                act.wait_ge(max_in, T + 1)
                wait_count(act, turned, 2 * (T - 3))
                act.activation(e[:, i % 4, :], neg[:, i % 2, :], ACT.Exp, bias=neg_max[:, v, i:i + 1],
                               scale=-1.0, accum_out=row_sum[:, v, i:i + 1]).then_inc(exp_in, 1)

            def take_turned(V, i):
                T, half = V * NT + i, i // TPH
                for g in range(2):
                    act.wait_ge(turned, 2 * T + g + 1)
                    act.activation(weights_t[:, half, g * TPH:(g + 1) * TPH, at(0, i % TPH, P)],
                                   turn[:, g, :].rearrange("p (t n) -> p t n", t=TPH), ACT.Copy).then_inc(turned_in, 1)

            def high_part(W, w):
                if not split:
                    return
                act.wait_ge(q_mm, W + 1)
                act.activation(q_high[w][:, :], S[:, query_slot(w), :], ACT.Copy).then_inc(q_high_in, 1)

            def take_destinations(W, w):
                if split:
                    return
                act.wait_ge(dst_mm, W + 1)
                wait_count(act, prod_in, (W - 1) * NT)
                act.activation(dst[:, w, :], S[:, w, :], ACT.Copy).then_inc(dst_in, 1)

            def take_mixed(V, half):
                act.wait_ge(mixed_mm, 2 * V + half + 1)
                act.activation(mixed[half][:, :], mix[:, :], ACT.Copy).then_inc(mixed_in, 1)

            def take_back(V, v, half):
                n = 2 * V + half
                if kind == HEAD_UNITS:
                    act.wait_ge(head_mm, n + 1)
                    act.activation(above[half][:, :], back[:, :], ACT.Relu, bias=b_now[v][:, 0:1])
                    act.activation(below[half][:, :], back[:, :], ACT.Relu, bias=b_now[v][:, 1:2],
                                   scale=-LEAK_HEADS).then_inc(biased, 1)
                else:
                    act.wait_ge(out_mm, n + 1)
                    out = res[:, half * TPH:(half + 1) * TPH, V, :] if isinstance(V, int) else \
                        res[:, half * TPH:(half + 1) * TPH, bass.ds(V, 1), :].rearrange("p t a c -> p t (a c)")
                    act.activation(out, back[:, 0:TPH * C].rearrange("p (t c) -> p t c", t=TPH), ACT.Copy).then_inc(out_in, 1)

            def behind(V, v, s):
                if s == AFTER0 - 1:
                    take_mixed(V, 0)
                if s == AFTER0 + 1:
                    take_back(V, v, 0)
                if s == AFTER1 - 1:
                    take_mixed(V, 1)

            def unit(U, u, V, V2):
                for s in range(NT):
                    more = not (isinstance(U, int) and U == units - 1)
                    if s == QUERY_TURN - 1 and more:
                        high_part(U + 1, 1 - u)
                    if s == 0 and V2 is not None:
                        take_back(V2, u, 1)
                    if V is not None:
                        behind(V, 1 - u, s)
                    W, same, i = lagged(U, V, s, LAG_TURN)
                    if W is not None:
                        take_turned(W, i)
                    W, same, i = lagged(U, V, s, LAG_EXP)
                    if W is not None:
                        exponent(W, u if same else 1 - u, i)
                    if s == 3 and more:
                        take_destinations(U + 1, 1 - u)

            high_part(0, 0)
            take_destinations(0, 0)

            def tail(V, V2):
                take_back(V2, 0, 1)
                for s in range(NT):
                    behind(V, 1, s)
                    if s == 0:
                        exponent(V, 1, NT - 1)
                    if s < LAG_TURN:
                        take_turned(V, s - LAG_TURN + NT)
                take_back(V, 1, 1)
            run(act, unit, tail)

        @block.gpsimd
        def _(pool):
            def normalise(V, v, i):
                wait_apart(pool, inv_in, V * NT + i + 1, pool_passed)
                pool.tensor_scalar(e[:, i % 4, :], e[:, i % 4, :], row_inv[:, v, i:i + 1], 1.0,
                                   ALU.mult, ALU.mult).then_inc(normed, 1)

            def copy(out, source):
                return pool.tensor_copy(out, source)

            def of_head(tensor, U):
                return tensor[:, U % HEADS]

            def copy_gram(W, w):
                if kind == HEAD_UNITS:
                    wait_apart(pool, q_mm, W - 1, pool_passed)
                    copy(gram[w][:, :, :], of_head(head_gram, W)).then_inc(gram_in, 1)

            def copy_head(W, w):
                if kind == HEAD_UNITS:
                    wait_apart(pool, out_mm, W - 1, pool_passed)
                    copy(w_now[w][:, :], of_head(head_w, W))
                    copy(ow_now[w][:, :], of_head(out_w, W))
                    copy(b_now[w][:, :], of_head(head_b, W)).then_inc(back_in, 1)

            def leaky(V, half):
                if kind == HEAD_UNITS:
                    pool.wait_ge(biased, 2 * V + half + 1)
                    pool.tensor_tensor(cat[half][:, :], above[half][:, :], below[half][:, :],
                                       ALU.subtract).then_inc(cat_in, 1)

            def unit(U, u, V, V2):
                for s in range(NT):
                    if s == 1 and V2 is not None:
                        leaky(V2, 1)
                    if s == AFTER0 + 2 and V is not None:
                        leaky(V, 0)
                    W, same, i = lagged(U, V, s, LAG_RECIP)
                    if W is not None:
                        normalise(W, u if same else 1 - u, i)
                    if s == 0 and not (isinstance(U, int) and U == units - 1):
                        copy_gram(U + 1, 1 - u)
                    if s == 4:
                        copy_head(U, u)

            copy_gram(0, 0)

            def tail(V, V2):
                for s in range(LAG_RECIP):
                    if s == 1:
                        leaky(V2, 1)
                    normalise(V, 1, s - LAG_RECIP + NT)
                leaky(V, 0)
                leaky(V, 1)
            run(pool, unit, tail)

        @block.sync
        def _(sync):
            def load(W, w):
                wait_count(sync, mixed_mm, 2 * (W - 1))
                sync.dma_start(val[w][:, :, :], values(batch(W))).then_inc(val_in[w], 16)
            load(0, 0)
            load(1, 1)
            with sync.Fori(2, units - 1, 2) as W:
                load(W, 0)
                load(W + 1, 1)


def layer_norm(nc, name, x_cur, res, finish, loads=()):
    GROUPS = 2
    ROWS = NT * B // GROUPS
    with ExitStack() as local:
        def sb(n, shape, dt=F32):
            return local.enter_context(nc.sbuf_tensor(f"{name}_{n}", shape, dt))

        def sem(n):
            return local.enter_context(nc.semaphore(f"{name}_{n}"))

        tmp = sb("tmp", [P, GROUPS, ROWS, C])
        mean = sb("mean", [P, GROUPS, ROWS])
        var = sb("var", [P, GROUPS, ROWS])
        std = sb("std", [P, GROUPS, ROWS])
        bias = sb("bias", [P, C])
        step, squared, rooted, centred = sem("step"), sem("squared"), sem("rooted"), sem("centred")
        if finish[0] == "elu":
            act_step, ready_for_exp = sem("act_step"), sem("ready_for_exp")
        if finish[0] == "leaky" or loads:
            loaded = sem("loaded")
        block = local.enter_context(nc.Block())
        rows = "p t b c -> p (t b) c"
        per = NT // GROUPS
        X = [x_cur[:, g * per:(g + 1) * per].rearrange(rows) for g in range(GROUPS)]
        R = [res[:, g * per:(g + 1) * per].rearrange(rows) for g in range(GROUPS)]

        def wide(a):
            return a.unsqueeze(2).broadcast_to([P, ROWS, C])

        @block.sync
        def _(sync):
            for out, source in [l for l in loads] + ([(bias[:, :], finish[1])] if finish[0] == "leaky" else []):
                sync.dma_start(out, source).then_inc(loaded, 16)

        n_loads = len(loads) + (finish[0] == "leaky")

        @block.vector
        def _(dve):
            count = [0]

            def then(ins):
                count[0] += 1
                ins.then_inc(step, 1)
                dve.wait_ge(step, count[0])

            if n_loads:
                dve.wait_ge(loaded, 16 * n_loads)
            for g in range(GROUPS):
                if finish[0] == "leaky":
                    then(dve.tensor_tensor(R[g], R[g], bias[:, :].unsqueeze(1).broadcast_to([P, ROWS, C]), ALU.add))
                    then(dve.scalar_tensor_tensor(out=R[g], in0=R[g], scalar=0.01, in1=R[g], op0=ALU.mult, op1=ALU.max))
                if finish[0] == "elu":
                    then(dve.tensor_scalar(tmp[:, g], R[g], 0.0, None, ALU.min))
                    dve.sem_inc(ready_for_exp, 1)
                    dve.wait_ge(act_step, g + 1)
                    then(dve.scalar_tensor_tensor(out=R[g], in0=R[g], scalar=0.0, in1=tmp[:, g], op0=ALU.max, op1=ALU.add))
                    then(dve.tensor_scalar(R[g], R[g], -1.0, None, ALU.add))
                then(dve.tensor_tensor(X[g], X[g], R[g], ALU.add))
                then(dve.tensor_reduce(mean[:, g], X[g], AX.X, ALU.add))
                then(dve.tensor_scalar(mean[:, g], mean[:, g], 1.0 / C, None, ALU.mult))
                then(dve.tensor_tensor(X[g], X[g], wide(mean[:, g]), ALU.subtract))
                dve.sem_inc(centred, 1)
                dve.wait_ge(squared, g + 1)
                then(dve.tensor_reduce(var[:, g], tmp[:, g], AX.X, ALU.add))
                then(dve.tensor_scalar(var[:, g], var[:, g], 1.0 / C, EPS, ALU.mult, ALU.add))
            for g in range(GROUPS):
                dve.wait_ge(rooted, g + 1)
                then(dve.reciprocal(std[:, g], std[:, g]))
                then(dve.tensor_tensor(X[g], X[g], wide(std[:, g]), ALU.mult))

        @block.scalar
        def _(act):
            for g in range(GROUPS):
                if finish[0] == "elu":
                    act.wait_ge(ready_for_exp, g + 1)
                    act.activation(tmp[:, g], tmp[:, g], ACT.Exp).then_inc(act_step, 1)
                act.wait_ge(centred, g + 1)
                act.activation(tmp[:, g], X[g], ACT.Square).then_inc(squared, 1)
            per_group = {"leaky": 2, "elu": 3, "none": 0}[finish[0]] + 6
            for g in range(GROUPS):
                act.wait_ge(step, per_group * (g + 1))
                act.activation(std[:, g], var[:, g], ACT.Sqrt).then_inc(rooted, 1)


def chebyshev(nc, k, x_cur, res, graph_t, embedding, weight, bias):
    with ExitStack() as local:
        def sb(name, shape, dt=F32):
            return local.enter_context(nc.sbuf_tensor(name, shape, dt))

        def sem(name):
            return local.enter_context(nc.semaphore(name))

        t1 = sb("t1", [P, NT, B * C])
        t2 = sb("t2", [P, NT, B * C])
        emb = sb("emb", [P, NT, EMB])
        emb_t = sb("emb_t", [EMB, NT, P])
        bias_in = sb("bias_in", [EMB, C])
        bias_now = sb("bias_now", [P, NT, C])
        w_whole = sb("w_whole", [P, ORDERS, EMB * C])
        w_part = [sb(f"w_part{i}", [P, ORDERS, EMB * C], F32R) for i in range(2)]
        joined = [sb(f"joined{i}", [P, B, ORDERS, 2, C], F32R) for i in range(2)]
        joined_t = [sb(f"joined_t{i}", [P, ORDERS, P], F32R) for i in range(2)]
        prods = w_whole[:, 0:2, :].rearrange("p a (d c) -> p a d c", c=C)
        banks = [local.enter_context(nc.psum_tensor(f"pc{i}", [P, HALF], F32))[:, :] for i in range(4)]
        y = local.enter_context(nc.psum_tensor("cheb_y", [P, 2, EMB * C], F32))
        w_in, w_high, w_low, g_turned, g_in = sem("w_inc"), sem("w_high"), sem("w_low"), sem("g_turned"), sem("g_inc")
        t_mm, t_in, e_mm, e_in = sem("t_mm"), sem("t_in"), sem("e_mmc"), sem("e_inc")
        high_in, join_in, join_mm, join_t_in = sem("high_inc"), sem("join_in"), sem("join_mm"), sem("join_t_in")
        y_mm, prod_in, sum_in = sem("y_mm"), sem("prod_inc"), sem("sum_in")
        pool_passed = sem("pool_passedc")
        block = local.enter_context(nc.Block())
        G_BANKS = NT * 2
        SOURCES = (x_cur.rearrange("p t b c -> p t (b c)"), t1, t2)

        @block.sync
        def _(sync):
            sync.dma_start(emb[:, :, :], embedding.rearrange("(t p) d -> p t d", p=P)).then_inc(w_in, 16)
            sync.dma_start(bias_in[:, :], bias).then_inc(w_in, 16)
            for order in range(ORDERS):
                for q in (0, C):
                    sync.dma_start(w_whole[q:q + C, order, :].rearrange("p (d o) -> p d o", d=EMB),
                                   weight[:, order].rearrange("d i o -> i d o")).then_inc(w_in, 16)

        @block.tensor
        def _(pe):
            for n in range(G_BANKS):
                mt, half = n // 2, n % 2
                wait_count(pe, g_in, n - 3)
                for t in range(TPH):
                    last = pe.transpose(banks[n % 4][:, at(0, t, P)], k["graph"][:, half * TPH + t, at(0, mt, P)],
                                        k["ident"][:, :])
                last.then_inc(g_turned, 1)
            pe.wait_ge(w_in, 128)
            for t in range(NT):
                last = pe.transpose(y[0:EMB, 0, at(0, t, P)], emb[:, t, :], k["ident"][:, :])
            last.then_inc(e_mm, 1)
            pe.wait_ge(g_in, G_BANKS)
            for order in range(2):
                for t in range(NT):
                    n = order * NT + t
                    wait_count(pe, t_in, n - 3 if t or not order else n)
                    for m in range(NT):
                        last = pe.matmul(banks[n % 4], graph_t[:, m, at(0, t, P)], SOURCES[order][:, m, :],
                                         start=m == 0, stop=m == NT - 1)
                    last.then_inc(t_mm, 1)
            pe.wait_ge(e_in, 1)
            for t in range(NT):
                last = pe.matmul(y[:, 1, at(0, t, C)], emb_t[:, t, :], bias_in[:, :], start=True, stop=True)
            last.then_inc(e_mm, 1)
            pe.wait_ge(t_in, 2 * NT)

            def turn(t, half, b):
                n = t * B + b
                if b == 0:
                    pe.wait_ge(join_in, t + 1)
                wait_count(pe, join_t_in, n - 1)
                for order in range(ORDERS):
                    last = pe.transpose(banks[b % 2][:, at(0, order, P)],
                                        joined[half][:, b, order].rearrange("p a c -> p (a c)").bitcast(F32),
                                        k["ident"][:, :])
                last.then_inc(join_mm, 1)

            def products(t, b):
                n = t * B + b
                pe.wait_ge(join_t_in, n + 1)
                wait_count(pe, prod_in, n - 1)
                for order in range(ORDERS):
                    for part in range(2):
                        for h in range(2):
                            last = pe.matmul(y[:, b % 2, at(0, h, HALF)], joined_t[b % 2][:, order, :],
                                             w_part[part][:, order, at(0, h, HALF)],
                                             start=order + part == 0, stop=order == ORDERS - 1 and part == 1)
                last.then_inc(y_mm, 1)

            def tile(t, half, more=True):
                for b in range(B):
                    if b < B - 1:
                        turn(t, half, b + 1)
                    elif more:
                        turn(t + 1, 1 - half, 0)
                    products(t, b)
            turn(0, 0, 0)
            pe.wait_ge(w_low, 1)
            pe.wait_ge(e_in, 2)
            tile(0, 0)
            with pe.Fori(1, NT - 2, 2) as t:
                tile(t, 1)
                tile(t + 1, 0)
            tile(NT - 1, 1, more=False)

        @block.scalar
        def _(act):
            for n in range(G_BANKS):
                act.wait_ge(g_turned, n + 1)
                act.activation(graph_t[:, n // 2, at(0, n % 2, HALF)], banks[n % 4], ACT.Copy).then_inc(g_in, 1)
            act.wait_ge(e_mm, 1)
            act.activation(emb_t[:, :, :], y[0:EMB, 0, :].rearrange("p (t n) -> p t n", t=NT), ACT.Copy).then_inc(e_in, 1)
            act.wait_ge(w_in, 128)
            act.activation(w_part[0][:, :, :], w_whole[:, :, :], ACT.Copy).then_inc(w_high, 1)
            act.wait_ge(e_mm, 2)
            act.activation(bias_now[:, :, :], y[:, 1, 0:NT * C].rearrange("p (t c) -> p t c", t=NT), ACT.Copy).then_inc(e_in, 1)

            def tile(t):
                for b in range(B):
                    n = t * B + b
                    act.wait_ge(join_mm, n + 1)
                    wait_count(act, y_mm, n - 1)
                    act.activation(joined_t[b % 2][:, :, :],
                                   banks[b % 2][:, 0:ORDERS * P].rearrange("p (j n) -> p j n", j=ORDERS),
                                   ACT.Copy).then_inc(join_t_in, 1)
            tile(0)
            with act.Fori(1, NT) as t:
                tile(t)

        @block.gpsimd
        def _(pool):
            pool.wait_ge(w_high, 1)
            pool.tensor_tensor(w_part[1][:, :, :], w_whole[:, :, :], w_part[0][:, :, :].bitcast(F32),
                               ALU.subtract).then_inc(w_low, 1)
            pool.wait_ge(t_in, 2 * NT)

            def join(t, half):
                wait_apart(pool, join_mm, (t - 1) * B, pool_passed)
                for order, source in enumerate(SOURCES):
                    pool.tensor_copy(joined[half][:, :, order, 0, :],
                                     source[:, t, :].rearrange("p (b c) -> p b c", b=B)).then_inc(high_in, 1)
                for order, source in enumerate(SOURCES):
                    wait_apart(pool, high_in, ORDERS * t + order + 1, pool_passed)
                    last = pool.tensor_tensor(joined[half][:, :, order, 1, :],
                                              source[:, t, :].rearrange("p (b c) -> p b c", b=B),
                                              joined[half][:, :, order, 0, :].bitcast(F32), ALU.subtract)
                last.then_inc(join_in, 1)

            def add_bias(t):
                wait_apart(pool, sum_in, (t + 1) * B, pool_passed)
                pool.tensor_tensor(res[:, t], res[:, t], bias_now[:, t, :].unsqueeze(1).broadcast_to([P, B, C]), ALU.add)
            join(0, 0)
            join(1, 1)
            pool.wait_ge(e_in, 2)
            with pool.Fori(2, NT - 1, 2) as t:
                join(t, 0)
                add_bias(t - 2)
                join(t + 1, 1)
                add_bias(t - 1)
            add_bias(NT - 2)
            add_bias(NT - 1)

        @block.vector
        def _(dve):
            for n in range(2 * NT):
                t = n % NT
                dve.wait_ge(t_mm, n + 1)
                if n < NT:
                    dve.tensor_copy(t1[:, t, :], banks[n % 4]).then_inc(t_in, 1)
                else:
                    dve.scalar_tensor_tensor(out=t2[:, t, :], in0=banks[n % 4], scalar=2.0,
                                             in1=x_cur[:, t].rearrange("p b c -> p (b c)"),
                                             op0=ALU.mult, op1=ALU.subtract).then_inc(t_in, 1)
            dve.wait_ge(w_in, 128)
            dve.wait_ge(w_low, 1)

            def product(t, b):
                n = t * B + b
                dve.wait_ge(y_mm, n + 1)
                wait_count(dve, sum_in, n - 1)
                dve.tensor_tensor(prods[:, b % 2], y[:, b % 2].rearrange("p (d c) -> p d c", c=C),
                                  emb[:, t, :].unsqueeze(2).broadcast_to([P, EMB, C]), ALU.mult).then_inc(prod_in, 1)

            def total(t, b):
                n = t * B + b
                dve.wait_ge(prod_in, n + 1)
                dve.tensor_reduce(res[:, t, b, :], prods[:, b % 2].rearrange("p d c -> p c d"), AX.X,
                                  ALU.add).then_inc(sum_in, 1)

            def tile(t, before):
                for b in range(B):
                    product(t, b)
                    if b:
                        total(t, b - 1)
                    elif before is not None:
                        total(before, B - 1)
            tile(0, None)
            with dve.Fori(1, NT) as t:
                tile(t, t - 1)
            total(NT - 1, B - 1)


def message_passing(nc, k, x_cur, res, graph_t, value, W1, b1, W2, b2):
    with ExitStack() as local:
        def sb(name, shape, dt=F32):
            return local.enter_context(nc.sbuf_tensor(name, shape, dt))

        def sem(name):
            return local.enter_context(nc.semaphore(name))

        v = sb("v", [P, NT, B * C])
        v_t = sb("v_t", [P, PAIRS, N])
        effect = [sb(f"effect{i}", [P, HALF]) for i in range(2)]
        hidden = [sb(f"hidden{i}", [P, HALF]) for i in range(2)]
        wn = sb("wn", [P, 3, P])
        wtr = sb("wtr", [P, 3, P])
        b1c, b2c = sb("b1c", [P, 1]), sb("b2c", [P, 1])
        b2r = sb("b2r", [P, C])
        banks = [local.enter_context(nc.psum_tensor(f"pm{i}", [P, HALF], F32))[:, :] for i in range(8)]
        e_bank, h_bank, n_bank, t_bank = banks[0:2], banks[2:4], banks[4:6], banks[6:8]
        cleared, w_in, v_in, v_set = sem("cleared3"), sem("w_in3"), sem("v_in3"), sem("v_set")
        turned, taken = sem("turned3"), sem("taken3")
        e_mm, e_in, h_mm, h_in = sem("e_mm"), sem("e_in"), sem("h_mm3"), sem("h_in3")
        n_mm, n_in, t_mm, t_in = sem("n_mm"), sem("n_in"), sem("t_mm3"), sem("t_in3")
        block = local.enter_context(nc.Block())
        SETUP = 1 + 2 * PAIRS
        KINDS = 2 * PAIRS

        @block.sync
        def _(sync):
            sync.wait_ge(cleared, 1)
            for q in range(2):
                d = slice(q * C, (q + 1) * C)
                for j, source in enumerate((W1[:, 0:C], W1[:, C:2 * C], W2)):
                    sync.dma_start(wn[d, j, d], source).then_inc(w_in, 16)
                sync.dma_start(b1c[d, :], b1.unsqueeze(1)).then_inc(w_in, 16)
                sync.dma_start(b2c[d, :], b2.unsqueeze(1)).then_inc(w_in, 16)
            sync.dma_start(b2r[:, :], b2.unsqueeze(0).broadcast_to([P, C])).then_inc(w_in, 16)
            sync.wait_ge(v_in, 1)
            sync.dma_start(v[0:1, 0, :].rearrange("p (b c) -> p b c", b=B),
                           value.unsqueeze(1).broadcast_to([1, B, C])).then_inc(v_set, 16)

        @block.gpsimd
        def _(pool):
            pool.memset(wn[:, :, :], 0.0).then_inc(cleared, 1)

        @block.tensor
        def _(pe):
            pe.wait_ge(w_in, 16 * 11)
            for j in range(3):
                last = pe.transpose(n_bank[0][:, at(0, j, P)], wn[:, j, :], k["ident"][:, :])
            last.then_inc(turned, 1)
            pe.wait_ge(v_set, 16)
            for g in range(2 * PAIRS):
                wait_count(pe, taken, g)
                for t in range(TPH):
                    last = pe.transpose(n_bank[(g + 1) % 2][:, at(0, t, P)],
                                        v[:, (g % 2) * TPH + t, at(0, g // 2, P)], k["ident"][:, :])
                last.then_inc(turned, 1)
            pe.wait_ge(taken, SETUP)

            def effects(r, g):
                pair, half = g // 2, g % 2
                n = r * KINDS + g
                if half == 0:
                    wait_count(pe, n_in, (r - 1) * KINDS + 2 * pair + 2)
                wait_count(pe, e_in, n - 1)
                for m in range(NT):
                    last = pe.matmul(e_bank[half], v[:, m, at(0, pair, P)], graph_t[:, m, at(0, half, HALF)],
                                     start=m == 0, stop=m == NT - 1)
                last.then_inc(e_mm, 1)

            def hiddens(r, g):
                pair, half = g // 2, g % 2
                n = r * KINDS + g
                wait_count(pe, t_in, (r - 1) * KINDS + g + 1)
                pe.wait_ge(e_in, n + 1)
                wait_count(pe, h_in, n - 1)
                pe.matmul(h_bank[half], wtr[:, 0, :], v_t[:, pair, at(0, half, HALF)], start=True, stop=False)
                pe.matmul(h_bank[half], wtr[:, 1, :], effect[half][:, :], start=False, stop=True).then_inc(h_mm, 1)

            def news(r, g):
                half = g % 2
                n = r * KINDS + g
                pe.wait_ge(h_in, n + 1)
                wait_count(pe, n_in, n - 1)
                for t in range(TPH):
                    last = pe.matmul(n_bank[half][:, at(0, t, P)], hidden[half][:, at(0, t, P)], wtr[:, 2, :],
                                     start=True, stop=True)
                last.then_inc(n_mm, 1)
                wait_count(pe, t_in, n - 1)
                pe.matmul(t_bank[half], wtr[:, 2, :], hidden[half][:, :], start=True, stop=True).then_inc(t_mm, 1)

            def step(r):
                for g in range(KINDS + 2):
                    if g < KINDS:
                        effects(r, g)
                    if 1 <= g <= KINDS:
                        hiddens(r, g - 1)
                    if g >= 2:
                        news(r, g - 2)
            step(0)
            with pe.Fori(1, STEPS) as r:
                step(r)

        @block.vector
        def _(dve):
            dve.tensor_copy(v[:, :, :], x_cur.rearrange("p t b c -> p t (b c)")).then_inc(v_in, 1)
            for g in range(SETUP):
                dve.wait_ge(turned, g + 1)
                if g == 0:
                    dve.tensor_copy(wtr[:, :, :], n_bank[0][:, 0:3 * P].rearrange("p (j n) -> p j n", j=3)).then_inc(taken, 1)
                else:
                    q = g - 1
                    dve.tensor_copy(v_t[:, q // 2, at(0, q % 2, HALF)], n_bank[g % 2]).then_inc(taken, 1)

            def step(r):
                for g in range(KINDS):
                    pair, half = g // 2, g % 2
                    n = r * KINDS + g
                    dve.wait_ge(n_mm, n + 1)
                    if half == 0:
                        dve.wait_ge(e_mm, n + 2)
                    dve.tensor_tensor(v[:, half * TPH:(half + 1) * TPH, at(0, pair, P)]
                                      .rearrange("p t (b c) -> p t b c", b=2),
                                      n_bank[half].rearrange("p (t b c) -> p t b c", t=TPH, b=2),
                                      b2r[:, :].unsqueeze(1).unsqueeze(1).broadcast_to([P, TPH, 2, C]),
                                      ALU.add).then_inc(n_in, 1)
            step(0)
            with dve.Fori(1, STEPS) as r:
                step(r)
            dve.wait_ge(n_in, STEPS * KINDS)
            dve.tensor_copy(res.rearrange("p t b c -> p t (b c)"), v[:, :, :])

        @block.scalar
        def _(act):
            act.wait_ge(w_in, 16 * 11)

            def step(r):
                for g in range(KINDS + 2):
                    if g < KINDS:
                        half, n = g % 2, r * KINDS + g
                        act.wait_ge(e_mm, n + 1)
                        wait_count(act, h_mm, n - 1)
                        act.activation(effect[half][:, :], e_bank[half], ACT.Copy).then_inc(e_in, 1)
                    if 1 <= g <= KINDS:
                        half, n = (g - 1) % 2, r * KINDS + g - 1
                        act.wait_ge(h_mm, n + 1)
                        wait_count(act, t_mm, n - 1)
                        act.activation(hidden[half][:, :], h_bank[half], ACT.Relu, bias=b1c[:, 0:1]).then_inc(h_in, 1)
                    if g >= 2:
                        pair, half, n = (g - 2) // 2, g % 2, r * KINDS + g - 2
                        act.wait_ge(t_mm, n + 1)
                        act.activation(v_t[:, pair, at(0, half, HALF)], t_bank[half], ACT.Identity,
                                       bias=b2c[:, 0:1]).then_inc(t_in, 1)
            step(0)
            with act.Fori(1, STEPS) as r:
                step(r)


def graph_stack(nc, x, adj, L0_gnn_Wh, L0_gnn_bh, L0_gnn_W_out, L0_gnn_b_out, L1_gnn_embedding, L1_gnn_weight,
                L1_gnn_bias, L2_gnn_intervention_value, L2_gnn_W1, L2_gnn_b1, L2_gnn_W2, L2_gnn_b2, L3_gnn_W,
                L3_gnn_a, out):
    with ExitStack() as ctx:
        k = constants(nc, ctx, adj)
        res = ctx.enter_context(nc.sbuf_tensor("res", [P, NT, B, C], F32))[:, :, :, :]
        xv = x.rearrange("b (t p) c -> p t b c", p=P)

        sums = res.rearrange("p t b c -> p t (b c)")
        with ExitStack() as layer:
            def sb(name, shape, dt=F32):
                return layer.enter_context(nc.sbuf_tensor(name, shape, dt))
            xs = sb("xs", [P, B, N], F32R)
            gram, head_w = sb("head_gram", [P, HEADS, 2, P], F32R), sb("head_w", [P, HEADS, HID])
            out_w, head_b = sb("out_w", [P, HEADS, C]), sb("head_b", [P, HEADS, 2])
            prepare_heads(nc, k, x, L0_gnn_Wh, L0_gnn_bh, L0_gnn_W_out, xs, gram, head_w, out_w, head_b, sums)

            def x_of(b):
                if isinstance(b, int):
                    return x[b].rearrange("(t p) c -> p t c", p=P)
                return x[bass.ds(b, 1)].rearrange("a (t p) c -> p (a t) c", p=P)
            attention(nc, k, HEAD_UNITS, x_of, sums, xs, gram, head_w, out_w, head_b)

        def values_of(tensor):
            def of(b):
                if isinstance(b, int):
                    return tensor[:, :, b, :]
                return tensor[:, :, bass.ds(b, 1), :].rearrange("p t a c -> p t (a c)")
            return of

        with ExitStack() as layer:
            xs = layer.enter_context(nc.sbuf_tensor("xs2", [P, B, N], F32R))
            nat = layer.enter_context(nc.sbuf_tensor("nat2", [P, NT, B, C], F32))
            prepare_output_head(nc, k, sums, xs, nat)
            attention(nc, k, OUTPUT_UNITS, values_of(nat), res, xs)

        x_cur_t = ctx.enter_context(nc.sbuf_tensor("x_cur", [P, NT, B, C], F32))
        x_cur = x_cur_t[:, :, :, :]
        layer_norm(nc, "norm1", x_cur, res, ("leaky", L0_gnn_b_out.unsqueeze(0).broadcast_to([P, C])),
                   [(x_cur[:, t], xv[:, t]) for t in range(NT)])

        with ExitStack() as layer:
            graph_t = layer.enter_context(nc.sbuf_tensor("graph_t", [P, NT, N], F32))
            chebyshev(nc, k, x_cur, res, graph_t, L1_gnn_embedding, L1_gnn_weight, L1_gnn_bias)
            layer_norm(nc, "norm2", x_cur, res, ("none",))
            message_passing(nc, k, x_cur, res, graph_t, L2_gnn_intervention_value, L2_gnn_W1, L2_gnn_b1,
                            L2_gnn_W2, L2_gnn_b2)
            layer_norm(nc, "norm3", x_cur, res, ("none",))

        with ExitStack() as layer:
            def sb(name, shape, dt=F32):
                return layer.enter_context(nc.sbuf_tensor(name, shape, dt))
            nat = sb("nat4", [P, NT, B, C])
            src_score, dst_w, x_pairs = sb("src_score", [P, B, NT]), sb("dst_w", [P, 2, P]), sb("x_pairs4", [P, PAIRS, N])
            prepare_edges(nc, k, x_cur.rearrange("p t b c -> p t (b c)"), L3_gnn_W, L3_gnn_a, nat, src_score, dst_w, x_pairs)
            attention(nc, k, EDGE_UNITS, values_of(nat), res, src_score=src_score, dst_w=dst_w, x_pairs=x_pairs)
        layer_norm(nc, "norm4", x_cur, res, ("elu",))

        with ExitStack() as local:
            stored = local.enter_context(nc.semaphore("stored"))
            block = local.enter_context(nc.Block())
            ov = out.rearrange("b (t p) c -> p t b c", p=P)

            @block.sync
            def _(sync):
                for t in range(NT):
                    sync.dma_start(ov[:, t], x_cur[:, t]).then_inc(stored, 16)
                sync.wait_ge(stored, 16 * NT)


_INS = ['x', 'adj', 'L0_gnn_Wh', 'L0_gnn_bh', 'L0_gnn_W_out', 'L0_gnn_b_out', 'L1_gnn_embedding', 'L1_gnn_weight',
        'L1_gnn_bias', 'L2_gnn_intervention_value', 'L2_gnn_W1', 'L2_gnn_b1', 'L2_gnn_W2', 'L2_gnn_b2', 'L3_gnn_W',
        'L3_gnn_a']


def kernel(**inputs):
    import numpy as np
    import concourse.bacc as bacc
    from concourse import mybir as _mybir
    from concourse.bass_utils import run_bass_kernel_spmd

    nc = bacc.Bacc("TRN2", target_bir_lowering=False, num_devices=1)
    arrays, args = {}, []
    for name in _INS:
        a = np.ascontiguousarray(inputs[name])
        arrays[f"in_{name}"] = a
        args.append(nc.dram_tensor(f"in_{name}", a.shape, _mybir.dt.from_np(a.dtype), kind="ExternalInput").ap())
    out = nc.dram_tensor("out_0", (B, N, C), F32, kind="ExternalOutput").ap()
    graph_stack(nc, *args, out)
    r = run_bass_kernel_spmd(nc, [arrays], core_ids=[0])
    return r.results[0]["out_0"]
```

```python
from contextlib import ExitStack

import concourse.bass as bass
from concourse import mybir

F32 = mybir.dt.float32
F32R = mybir.dt.float32r
ALU = mybir.AluOpType
ACT = mybir.ActivationFunctionType
AX = mybir.AxisListType

P = 128
B = 8
N = 1024
C = 64
HEADS = 8
HID = 128
NT = N // P
HALF = N // 2
PAIRS = B // 2
TPH = NT // 2
EMB = 16
ORDERS = 3
STEPS = 3
LEAK_HEADS = 0.01
NEG_HEADS = -1e16
NEG_EDGES = -9000000000000000.0
BIG = 3.0e38
EPS = 1e-5


def wait_count(engine, sem, value):
    if isinstance(value, int) and value <= 0:
        return
    engine.wait_ge(sem, value)


def wait_apart(engine, sem, value, passed):
    if isinstance(value, int):
        wait_count(engine, sem, value)
    else:
        engine.wait_ge(sem, value)
        engine.sem_inc(passed, 1)


def at(base, index, size):
    if isinstance(index, int):
        return slice(base + index * size, base + (index + 1) * size)
    return bass.ds(index * size + base, size)


def constants(nc, ctx):
    def sb(name, shape, dt=F32):
        return ctx.enter_context(nc.sbuf_tensor(name, shape, dt))

    k = {
        "ident": sb("ident", [P, P]),
        "dup0": sb("dup0", [P, P]),
        "dup1": sb("dup1", [P, P]),
        "dups": sb("dups", [P, P]),
        "dups_r": sb("dups_r", [P, P], F32R),
        "graph": sb("graph", [P, NT, N]),
    }
    with ExitStack() as local:
        def sem(name):
            return local.enter_context(nc.semaphore(name))
        cleared, ident_made, dup_made = sem("cleared"), sem("ident_made"), sem("dup_made")
        block = local.enter_context(nc.Block())

        @block.gpsimd
        def _(pool):
            pool.memset(k["ident"][:, :], 0.0).then_inc(cleared, 1)
            pool.wait_ge(cleared, 1)
            pool.affine_select(out=k["ident"][:, :], in_=k["ident"][:, :], compare_op=ALU.not_equal, fill=1.0,
                               base=0, pattern=[[-1, P]], channel_multiplier=1).then_inc(ident_made, 1)

        @block.vector
        def _(dve):
            dve.wait_ge(ident_made, 1)
            for col in (0, C):
                dve.tensor_copy(k["dup0"][:, col:col + C], k["ident"][:, 0:C]).then_inc(dup_made, 1)
                dve.tensor_copy(k["dup1"][:, col:col + C], k["ident"][:, C:P]).then_inc(dup_made, 1)
            dve.wait_ge(dup_made, 4)
            for dups in ("dups", "dups_r"):
                dve.tensor_tensor(k[dups][:, :], k["dup0"][:, :], k["dup1"][:, :], ALU.add)
    return k


def stack_parts(block, stacked, banks, fill, stacked_mm, high_in, low_in):
    slots = len(banks)
    BLOCKS = [(b, half) for half in range(2) for b in range(B)]

    @block.tensor
    def _(pe):
        for n, (b, half) in enumerate(BLOCKS):
            wait_count(pe, low_in, n - slots + 1)
            fill(pe, banks[n % slots], b, half).then_inc(stacked_mm, 1)

    @block.scalar
    def _(act):
        for n, (b, half) in enumerate(BLOCKS):
            act.wait_ge(stacked_mm, n + 1)
            act.activation(stacked[:, b, at(0, half, HALF)], banks[n % slots], ACT.Copy).then_inc(high_in, 1)

    @block.vector
    def _(dve):
        for n, (b, half) in enumerate(BLOCKS):
            low = stacked[C:P, b, at(0, half, HALF)]
            dve.wait_ge(high_in, n + 1)
            dve.tensor_tensor(low, banks[n % slots][C:P, :], low.bitcast(F32), ALU.subtract).then_inc(low_in, 1)


def prepare_heads(nc, k, x, adj, Wh, bh, W_out, xs, head_gram, head_w, out_w, head_b, sums):
    with ExitStack() as local:
        def sb(name, shape, dt=F32):
            return local.enter_context(nc.sbuf_tensor(name, shape, dt))

        def sem(name):
            return local.enter_context(nc.semaphore(name))

        x_nat = sb("x_nat", [P, NT, B, 2, C])
        wt = sb("wt", [P, HEADS, P])
        banks = [local.enter_context(nc.psum_tensor(f"ph{i}", [P, HALF], F32))[:, :] for i in range(8)]
        w_in, x_in, graph_in = sem("w_in"), [sem(f"x_in{i}") for i in range(2)], sem("graph_in")
        turned, taken, doubled = sem("turned"), sem("taken"), [sem(f"doubled{i}") for i in range(2)]
        stacked_mm, high_in, low_in = sem("stacked_mm"), sem("high_in"), sem("low_in")
        block = local.enter_context(nc.Block())
        W_BANKS = HEADS // 4

        @block.sync
        def _(sync):
            for copy in (0, C):
                sync.dma_start(head_w[copy:copy + C, :, :], Wh.rearrange("h c d -> c h d")).then_inc(w_in, 16)
            sync.dma_start(head_b[:, :, 0], bh.rearrange("h d -> d h"), allow_slow_non_contiguous=True).then_inc(w_in, 16)
            xv = x.rearrange("b (t p) c -> p t b c", p=P)
            for t in range(NT):
                sync.dma_start(x_nat[:, t, :, 0, :], xv[:, t]).then_inc(x_in[t // TPH], 16)
            gv = adj.rearrange("(t p) m -> p t m", p=P)
            for t in range(NT):
                sync.dma_start(k["graph"][:, t, :], gv[:, t]).then_inc(graph_in, 16)
            sync.dma_start(out_w[:, :, :], W_out.rearrange("(h d) o -> d h o", d=HID)).then_inc(graph_in, 16)
            sync.wait_ge(graph_in, 16 * (NT + 1))

        @block.tensor
        def _(pe):
            pe.wait_ge(w_in, 48)
            for h in range(HEADS):
                last = pe.transpose(banks[h // 4][:, at(0, h % 4, P)], head_w[:, h, :], k["ident"][:, :])
                if h % 4 == 3:
                    last.then_inc(turned, 1)
            for h in range(HEADS):
                if h % 4 == 0:
                    pe.wait_ge(taken, h // 4 + 1)
                last = pe.matmul(banks[h // 4][:, at(0, h % 4, P)], wt[:, h, :], wt[:, h, :], start=True, stop=True)
                if h % 4 == 3:
                    last.then_inc(turned, 1)

        @block.vector
        def _(dve):
            dve.wait_ge(w_in, 48)
            dve.tensor_scalar(head_b[:, :, 1], head_b[:, :, 0], -LEAK_HEADS, None, ALU.mult)
            for g in range(W_BANKS):
                dve.wait_ge(turned, g + 1)
                dve.tensor_copy(wt[:, 4 * g:4 * g + 4, :],
                                banks[g].rearrange("p (h d) -> p h d", h=4)).then_inc(taken, 1)
            for g in range(W_BANKS):
                dve.wait_ge(turned, W_BANKS + g + 1)
                high, low = (head_gram[:, 4 * g:4 * g + 4, part, :] for part in range(2))
                gram = banks[g].rearrange("p (h d) -> p h d", h=4)
                dve.tensor_copy(high, gram).then_inc(taken, 1)
                dve.wait_ge(taken, W_BANKS + g + 1)
                dve.tensor_tensor(low, gram, high.bitcast(F32), ALU.subtract)

        @block.gpsimd
        def _(pool):
            pool.memset(sums[:, :, :], 0.0)
            pool.wait_ge(x_in[1], 16 * TPH)
            for t in range(TPH, NT):
                pool.tensor_copy(x_nat[:, t, :, 1, :], x_nat[:, t, :, 0, :]).then_inc(doubled[1], 1)

        @block.scalar
        def _(act):
            act.wait_ge(x_in[0], 16 * TPH)
            for t in range(TPH):
                act.activation(x_nat[:, t, :, 1, :], x_nat[:, t, :, 0, :], ACT.Copy).then_inc(doubled[0], 1)

        def fill(pe, bank, b, half):
            if b == 0:
                pe.wait_ge(doubled[half], TPH)
            for t in range(TPH):
                last = pe.transpose(bank[:, at(0, t, P)],
                                    x_nat[:, half * TPH + t, b].rearrange("p a c -> p (a c)"), k["ident"][:, :])
            return last

        stack_parts(block, xs, banks[W_BANKS:8], fill, stacked_mm, high_in, low_in)


def prepare_output_head(nc, k, sums, xs, nat, loads):
    with ExitStack() as local:
        def sem(name):
            return local.enter_context(nc.semaphore(name))

        banks = [local.enter_context(nc.psum_tensor(f"po{i}", [P, HALF], F32))[:, :] for i in range(8)]
        turned, taken, loaded = sem("turned2"), sem("taken2"), sem("loaded2")
        stacked_mm, high_in, low_in = sem("stacked_mm2"), sem("high_in2"), sem("low_in2")
        block = local.enter_context(nc.Block())

        @block.sync
        def _(sync):
            for out, source in loads:
                sync.dma_start(out, source).then_inc(loaded, 16)
            sync.wait_ge(loaded, 16 * len(loads))

        @block.tensor
        def _(pe):
            for b in range(B):
                wait_count(pe, taken, b - 3)
                for t in range(TPH):
                    last = pe.transpose(banks[b % 4][:, at(0, t, P)], sums[:, b, at(0, t, P)], k["ident"][:, :])
                last.then_inc(turned, 1)

        @block.vector
        def _(dve):
            for b in range(B):
                dve.wait_ge(turned, b + 1)
                dve.tensor_copy(nat[:, :, b, :].rearrange("p (h t) c -> p t h c", h=2),
                                banks[b % 4].rearrange("p (t h c) -> p t h c", t=TPH, h=2)).then_inc(taken, 1)

        def fill(pe, bank, b, half):
            return pe.matmul(bank, k[f"dup{half}"][:, :], sums[:, b, :], start=True, stop=True)

        stack_parts(block, xs, banks[4:8], fill, stacked_mm, high_in, low_in)


def edge_weights(w2, a4, W, a):
    weights = []
    for q in range(2):
        d = slice(q * C, (q + 1) * C)
        weights += [(w2[d, d], W), (a4[d, q:q + 1], a[0:C, :]), (a4[d, 2 + q:3 + q], a[C:2 * C, :])]
    return {"clears": [w2[:, :], a4[:, :]], "weights": weights}


def prepare_edges(nc, k, x_cur, w2, a4, nat, src_score, dst_w, x_pairs):
    with ExitStack() as local:
        def sb(name, shape, dt=F32):
            return local.enter_context(nc.sbuf_tensor(name, shape, dt))

        def sem(name):
            return local.enter_context(nc.semaphore(name))

        WIDE = P + 2
        w2t = sb("w2t", [P, P])
        wa = sb("wa", [P, 4])
        ones = sb("ones", [P, P])
        banks = [local.enter_context(nc.psum_tensor(f"pe{i}", [P, HALF], F32))[:, :] for i in range(8)]
        cleared, turned, taken, made = sem("cleared4"), sem("turned4"), sem("taken4"), sem("made4")
        h_mm, h_in, masked = sem("h_mm"), sem("h_in"), sem("masked4")
        block = local.enter_context(nc.Block())

        @block.gpsimd
        def _(pool):
            pool.memset(ones[:, :], 1.0).then_inc(cleared, 1)

        @block.tensor
        def _(pe):
            pe.transpose(banks[0][:, 0:P], w2[:, 0:P], k["ident"][:, :]).then_inc(turned, 1)
            for g in range(2 * PAIRS):
                bank = banks[(1 + g) % 8]
                wait_count(pe, taken, g - 6)
                for t in range(TPH):
                    last = pe.transpose(bank[:, at(0, t, P)], x_cur[:, (g % 2) * TPH + t, at(0, g // 2, P)],
                                        k["ident"][:, :])
                last.then_inc(turned, 1)
            pe.wait_ge(taken, 1 + 2 * PAIRS)
            pe.matmul(banks[0][:, 0:4], w2t[:, :], a4[:, :], start=True, stop=True).then_inc(turned, 1)
            pe.wait_ge(made, 1)
            for n in range(PAIRS * NT):
                wait_count(pe, h_in, n - 3)
                pe.matmul(banks[1 + n % 4][:, 0:WIDE], x_pairs[:, n // NT, at(0, n % NT, P)], w2[:, :],
                          start=True, stop=True).then_inc(h_mm, 1)

        @block.vector
        def _(dve):
            dve.wait_ge(turned, 1)
            dve.tensor_copy(w2t[:, :], banks[0][:, 0:P]).then_inc(taken, 1)
            for g in range(2 * PAIRS):
                dve.wait_ge(turned, g + 2)
                dve.tensor_copy(x_pairs[:, g // 2, at(0, g % 2, HALF)], banks[(1 + g) % 8]).then_inc(taken, 1)
            dve.wait_ge(turned, 2 + 2 * PAIRS)
            dve.tensor_copy(wa[:, :], banks[0][:, 0:4]).then_inc(taken, 1)
            dve.wait_ge(taken, 2 + 2 * PAIRS)
            dve.tensor_copy(w2[:, P:WIDE], wa[:, 0:2]).then_inc(made, 1)
            dve.wait_ge(cleared, 1)
            for q in range(2):
                dve.tensor_scalar(dst_w[:, q, :], ones[:, :], wa[:, 2 + q:3 + q], None, ALU.mult)
            for t in range(NT):
                dve.tensor_scalar(k["graph"][:, t, :], k["graph"][:, t, :], 0.5, NEG_EDGES, ALU.is_le, ALU.mult)

        @block.scalar
        def _(act):
            for n in range(PAIRS * NT):
                pair, t = n // NT, n % NT
                bank = banks[1 + n % 4]
                act.wait_ge(h_mm, n + 1)
                act.activation(nat[:, t, 2 * pair:2 * pair + 2, :],
                               bank[:, 0:P].rearrange("p (b c) -> p b c", b=2), ACT.Copy)
                act.activation(src_score[:, 2 * pair:2 * pair + 2, t], bank[:, P:WIDE], ACT.Copy).then_inc(h_in, 1)


QUERY_TURN = 4
HEAD_UNITS, OUTPUT_UNITS, EDGE_UNITS = "heads", "output", "edges"
LAG_EXP, LAG_RECIP, LAG_TURN = 1, 2, 3
HALF0_TILES = {0: (0, 2), 1: (2, 6), 2: (6, 8)}
HALF1_TILES = {4: (0, 4), 5: (4, 6), 6: (6, 8)}
AFTER0, AFTER1 = 3, 7


def attention(nc, k, kind, values, res, xs=None, head_gram=None, head_w=None, out_w=None, head_b=None,
              src_score=None, dst_w=None, x_pairs=None):
    units = B * HEADS if kind == HEAD_UNITS else B
    split = kind != EDGE_UNITS
    LOW_PARTS = 2 if kind == HEAD_UNITS else 1

    def batch(U):
        return U // HEADS if kind == HEAD_UNITS else U

    with ExitStack() as local:
        def sb(name, shape, dt=F32):
            return local.enter_context(nc.sbuf_tensor(f"{kind}_{name}", shape, dt))

        def psum(name, shape):
            return local.enter_context(nc.psum_tensor(f"{kind}_{name}", shape, F32))

        def sem(name):
            return local.enter_context(nc.semaphore(f"{kind}_{name}"))

        S = psum("S", [P, 2, N])
        turn = psum("turn", [P, 2, HALF])
        mix = psum("mix", [P, HALF])
        back = psum("back", [P, HALF])

        prod = sb("prod", [P, 2, N])
        floor = sb("floor", [P, 2, N], mybir.dt.bfloat16 if split else F32)
        neg = sb("neg", [P, 2, N])
        e = sb("e", [P, 4, N])
        neg_max = sb("neg_max", [P, 2, NT])
        row_sum = sb("row_sum", [P, 2, NT])
        row_inv = sb("row_inv", [P, 2, NT])
        weights_t = sb("weights_t", [P, 2, NT, HALF])
        val = [sb(f"val{i}", [P, NT, C]) for i in range(2)]
        mixed = [sb(f"mixed{i}", [P, HALF]) for i in range(2)]
        if split:
            q_high = [sb(f"q_high{i}", [P, N], F32R) for i in range(2)]
            q_low = [sb(f"q_low{i}", [P, N], F32R) for i in range(2)]
        else:
            dst = sb("dst", [P, 2, N])
            src = sb("src", [P, 2, NT])
        if kind == HEAD_UNITS:
            q_whole = sb("q_whole", [P, HALF])
            gram = [sb(f"gram{i}", [P, 2, P], F32R) for i in range(2)]
            w_now = [sb(f"w_now{i}", [P, HID]) for i in range(2)]
            ow_now = [sb(f"ow_now{i}", [P, C]) for i in range(2)]
            b_now = [sb(f"b_now{i}", [P, 2]) for i in range(2)]
            above = [sb(f"above{i}", [P, HALF]) for i in range(2)]
            below = [sb(f"below{i}", [P, HALF]) for i in range(2)]
            cat = [sb(f"cat{i}", [P, HALF]) for i in range(2)]

        val_in = [sem(f"val_in{i}") for i in range(2)]
        if split:
            q_mm, q_high_in, q_low_in, scored = sem("q_mm"), sem("q_high_in"), sem("q_low_in"), sem("scored")
        else:
            dst_mm, dst_in, src_in = sem("dst_mm"), sem("dst_in"), sem("src_in")
        if kind == HEAD_UNITS:
            q_whole_in = sem("q_whole_in")
            gram_in, back_in = sem("gram_in"), sem("back_in")
            head_mm, biased, cat_in = sem("head_mm"), sem("biased"), sem("cat_in")
        prod_in, floor_in, max_in = sem("prod_in"), sem("floor_in"), sem("max_in")
        exp_in, inv_in, normed = sem("exp_in"), sem("inv_in"), sem("normed")
        turned, turned_in = sem("turned"), sem("turned_in")
        mixed_mm, mixed_in = sem("mixed_mm"), sem("mixed_in")
        out_mm, out_in = sem("out_mm"), sem("out_in")
        dve_passed, pool_passed = sem("dve_passed"), sem("pool_passed")
        block = local.enter_context(nc.Block())

        def run(engine, unit, tail):
            unit(0, 0, None, None)
            unit(1, 1, 0, None)
            with engine.Fori(2, units - 3, 2) as U:
                unit(U, 0, U - 1, U - 2)
                unit(U + 1, 1, U, U - 1)
            unit(units - 2, 0, units - 3, units - 4)
            unit(units - 1, 1, units - 2, units - 3)
            tail(units - 1, units - 2)

        def lagged(U, V, s, lag):
            return (U, True, s - lag) if s >= lag else (V, False, s - lag + NT)

        def slot_of(u, i):
            return (u + i + (i >= QUERY_TURN)) % 2

        def query_slot(w):
            return (1 - w + QUERY_TURN) % 2

        @block.tensor
        def _(pe):
            def queries(W, w):
                if not split:
                    return
                slot = S[:, query_slot(w), :]
                if kind == HEAD_UNITS:
                    pe.wait_ge(gram_in, W + 1)
                wait_count(pe, prod_in, (W - 1) * NT + QUERY_TURN - 1)
                parts = [gram[w][:, part, :] for part in range(2)] if kind == HEAD_UNITS else [k["dups_r"][:, :]]
                for n, part in enumerate(parts):
                    for half in range(2):
                        last = pe.matmul(slot[:, at(0, half, HALF)], part, xs[:, batch(W), at(0, half, HALF)],
                                         start=n == 0, stop=n == len(parts) - 1)
                last.then_inc(q_mm, 1)

            def destinations(W, w, q):
                wait_count(pe, dst_in, W - 1)
                for half in range(2):
                    last = pe.matmul(S[:, w, at(0, half, HALF)], dst_w[:, q, :],
                                     x_pairs[:, W // 2, at(0, half, HALF)], start=True, stop=True)
                last.then_inc(dst_mm, 1)

            def scores(U, u, i):
                if not split:
                    return
                if i == 0:
                    pe.wait_ge(q_low_in, LOW_PARTS * (U + 1))
                if i == QUERY_TURN + 1 and not (isinstance(U, int) and U == units - 1):
                    pe.wait_ge(q_low_in, LOW_PARTS * (U + 2))
                wait_count(pe, prod_in, U * NT + (i if i == QUERY_TURN else i - 1))
                for n, part in enumerate((q_high, q_low)):
                    for half in range(2):
                        last = pe.matmul(S[:, slot_of(u, i), at(0, half, HALF)], part[u][:, at(0, i, P)],
                                         xs[:, batch(U), at(0, half, HALF)], start=n == 0, stop=n == 1)
                last.then_inc(scored, 1)

            def transposes(V, i):
                T = V * NT + i
                pe.wait_ge(normed, T + 1)
                for g in range(2):
                    wait_count(pe, turned_in, 2 * T + g - 1)
                    for j in range(TPH):
                        last = pe.transpose(turn[:, g, at(0, j, P)], e[:, i % 4, at(0, g * TPH + j, P)],
                                            k["ident"][:, :])
                    last.then_inc(turned, 1)

            def mixing(V, v, half, first, end):
                if first == 0:
                    pe.wait_ge(turned_in, 2 * (V * NT + (half + 1) * TPH))
                    if half == 0:
                        pe.wait_ge(val_in[v], 16 * (V // 2 + 1))
                for t in range(first, end):
                    rows = slice(C * (t % 2), C * (t % 2) + C)
                    last = pe.matmul(mix[rows, :], val[v][:, t, :], weights_t[:, half, t, :],
                                     start=t < 2, stop=t >= NT - 2)
                if end == NT:
                    last.then_inc(mixed_mm, 1)

            def after(V, v, half):
                n = 2 * V + half
                pe.wait_ge(mixed_in, n + 1)
                if kind == HEAD_UNITS:
                    if half == 0:
                        pe.wait_ge(back_in, V + 1)
                        pe.wait_ge(out_in, V + 1)
                    else:
                        pe.wait_ge(biased, n)
                    pe.matmul(back[:, :], w_now[v][:, :], mixed[half][:, :], start=True, stop=True).then_inc(head_mm, 1)
                else:
                    for t in range(TPH):
                        last = pe.matmul(back[:, at(0, t, C)], mixed[half][:, at(0, t, P)], k["dups"][:, 0:C],
                                         start=True, stop=True)
                    last.then_inc(out_mm, 1)

            def outputs(V, v):
                if kind != HEAD_UNITS:
                    return
                pe.wait_ge(cat_in, 2 * V + 2)
                for half in range(2):
                    last = pe.matmul(back[half * C:half * C + C, :], ow_now[v][:, :], cat[half][:, :],
                                     start=True, stop=True)
                last.then_inc(out_mm, 1)

            def behind(V, v, s):
                if s in HALF0_TILES:
                    mixing(V, v, 0, *HALF0_TILES[s])
                if s in HALF1_TILES:
                    mixing(V, v, 1, *HALF1_TILES[s])

            def behind_turned(V, v, s):
                if s == AFTER0:
                    after(V, v, 0)
                if s == AFTER1:
                    after(V, v, 1)

            def unit(U, u, V, V2):
                more = not (isinstance(U, int) and U == units - 1)
                for s in range(NT):
                    scores(U, u, s)
                    if s == QUERY_TURN - 1 and more:
                        queries(U + 1, 1 - u)
                    if V is not None:
                        behind(V, 1 - u, s)
                    if s == 2 and V2 is not None:
                        outputs(V2, u)
                    W, _, i = lagged(U, V, s, LAG_TURN)
                    if W is not None:
                        transposes(W, i)
                    if V is not None:
                        behind_turned(V, 1 - u, s)
                    if s == 2 and more and not split:
                        destinations(U + 1, 1 - u, 1 - u)

            queries(0, 0)
            if not split:
                destinations(0, 0, 0)

            def tail(V, V2):
                for s in range(NT):
                    if s == 2:
                        outputs(V2, 0)
                    behind(V, 1, s)
                    if s < LAG_TURN:
                        transposes(V, s - LAG_TURN + NT)
                    behind_turned(V, 1, s)
                outputs(V, 1)
            run(pe, unit, tail)

        @block.vector
        def _(dve):
            def masking(U, u, i):
                T = U * NT + i
                wait_count(dve, max_in, T - 1)
                if split:
                    dve.wait_ge(scored, T + 1)
                    dve.tensor_tensor(prod[:, i % 2, :], S[:, slot_of(u, i), :], k["graph"][:, i, :],
                                      ALU.mult).then_inc(prod_in, 1)
                else:
                    if i == 0:
                        dve.wait_ge(dst_in, U + 1)
                        dve.tensor_copy(src[:, u, :], src_score[:, batch(U), :] if isinstance(U, int) else
                                        src_score[:, bass.ds(U, 1), :].rearrange("p a t -> p (a t)")).then_inc(src_in, 1)
                        dve.wait_ge(src_in, U + 1)
                    dve.tensor_scalar(prod[:, i % 2, :], dst[:, u, :], src[:, u, i:i + 1], None,
                                      ALU.add).then_inc(prod_in, 1)

            def flooring(U, i):
                T = U * NT + i
                dve.wait_ge(prod_in, T + 1)
                wait_count(dve, max_in, T - 1)
                if split:
                    dve.tensor_scalar(floor[:, i % 2, :], prod[:, i % 2, :], 0.0, NEG_HEADS,
                                      ALU.is_equal, ALU.mult).then_inc(floor_in, 1)
                else:
                    dve.scalar_tensor_tensor(out=floor[:, i % 2, :], in0=prod[:, i % 2, :], scalar=0.2,
                                             in1=prod[:, i % 2, :], op0=ALU.mult, op1=ALU.max).then_inc(floor_in, 1)

            def maximum(V, v, i):
                T = V * NT + i
                wait_count(dve, floor_in, T + 1)
                wait_apart(dve, exp_in, T - 1, dve_passed)
                if split:
                    in0, in1 = prod[:, i % 2, :], floor[:, i % 2, :]
                else:
                    in0, in1 = floor[:, i % 2, :], k["graph"][:, i, :]
                dve.tensor_tensor_reduce(neg[:, i % 2, :], in0, in1, -1.0, BIG, ALU.add, ALU.min,
                                         neg_max[:, v, i:i + 1]).then_inc(max_in, 1)

            def inverse(V, v, i):
                dve.wait_ge(exp_in, V * NT + i + 1)
                dve.reciprocal(row_inv[:, v, i:i + 1], row_sum[:, v, i:i + 1]).then_inc(inv_in, 1)

            def low_part(W, w):
                if not split:
                    return
                dve.wait_ge(q_high_in, W + 1)
                half = slice(0, N // LOW_PARTS)
                dve.tensor_tensor(q_low[w][:, half], S[:, query_slot(w), half], q_high[w][:, half].bitcast(F32),
                                  ALU.subtract).then_inc(q_low_in, 1)

            def add_heads(V):
                if kind != HEAD_UNITS:
                    return
                dve.wait_ge(out_mm, V + 1)
                dve.wait_ge(out_in, V + 1)
                dve.tensor_tensor(res[:, batch(V), :], res[:, batch(V), :], back[:, :], ALU.add).then_inc(out_in, 1)

            def unit(U, u, V, V2):
                for s in range(NT):
                    masking(U, u, s)
                    W, same, i = lagged(U, V, s, LAG_RECIP)
                    if W is not None:
                        inverse(W, u if same else 1 - u, i)
                    if s == QUERY_TURN and not (isinstance(U, int) and U == units - 1):
                        low_part(U + 1, 1 - u)
                    W, same, i = lagged(U, V, s, LAG_EXP)
                    if W is not None:
                        maximum(W, u if same else 1 - u, i)
                    flooring(U, s)
                    if s == 2 and V2 is not None:
                        add_heads(V2)

            if kind == HEAD_UNITS:
                dve.sem_inc(out_in, 1)
            low_part(0, 0)

            def tail(V, V2):
                for s in range(LAG_RECIP):
                    if s == 0:
                        maximum(V, 1, NT - 1)
                    inverse(V, 1, s - LAG_RECIP + NT)
                add_heads(V2)
                add_heads(V)
            run(dve, unit, tail)

        @block.scalar
        def _(act):
            def exponent(V, v, i):
                T = V * NT + i
                act.wait_ge(max_in, T + 1)
                wait_count(act, turned, 2 * (T - 3))
                act.activation(e[:, i % 4, :], neg[:, i % 2, :], ACT.Exp, bias=neg_max[:, v, i:i + 1],
                               scale=-1.0, accum_out=row_sum[:, v, i:i + 1]).then_inc(exp_in, 1)

            def take_turned(V, i):
                T, half = V * NT + i, i // TPH
                for g in range(2):
                    act.wait_ge(turned, 2 * T + g + 1)
                    act.activation(weights_t[:, half, g * TPH:(g + 1) * TPH, at(0, i % TPH, P)],
                                   turn[:, g, :].rearrange("p (t n) -> p t n", t=TPH), ACT.Copy).then_inc(turned_in, 1)

            def high_part(W, w):
                if not split:
                    return
                act.wait_ge(q_mm, W + 1)
                act.activation(q_high[w][:, :], S[:, query_slot(w), :], ACT.Copy).then_inc(q_high_in, 1)
                if kind == HEAD_UNITS:
                    wait_count(act, q_low_in, 2 * W)
                    act.activation(q_whole[:, :], S[:, query_slot(w), HALF:N], ACT.Copy).then_inc(q_whole_in, 1)

            def take_destinations(W, w):
                if split:
                    return
                act.wait_ge(dst_mm, W + 1)
                wait_count(act, prod_in, (W - 1) * NT)
                act.activation(dst[:, w, :], S[:, w, :], ACT.Copy).then_inc(dst_in, 1)

            def take_mixed(V, half):
                act.wait_ge(mixed_mm, 2 * V + half + 1)
                act.activation(mixed[half][:, :], mix[:, :], ACT.Copy).then_inc(mixed_in, 1)

            def take_back(V, v, half):
                n = 2 * V + half
                if kind == HEAD_UNITS:
                    act.wait_ge(head_mm, n + 1)
                    act.activation(above[half][:, :], back[:, :], ACT.Relu, bias=b_now[v][:, 0:1])
                    act.activation(below[half][:, :], back[:, :], ACT.Relu, bias=b_now[v][:, 1:2],
                                   scale=-LEAK_HEADS).then_inc(biased, 1)
                else:
                    act.wait_ge(out_mm, n + 1)
                    out = res[:, half * TPH:(half + 1) * TPH, V, :] if isinstance(V, int) else \
                        res[:, half * TPH:(half + 1) * TPH, bass.ds(V, 1), :].rearrange("p t a c -> p t (a c)")
                    act.activation(out, back[:, 0:TPH * C].rearrange("p (t c) -> p t c", t=TPH), ACT.Copy).then_inc(out_in, 1)

            def behind(V, v, s):
                if s == AFTER0 - 1:
                    take_mixed(V, 0)
                if s == AFTER0 + 1:
                    take_back(V, v, 0)
                if s == AFTER1 - 1:
                    take_mixed(V, 1)

            def unit(U, u, V, V2):
                for s in range(NT):
                    more = not (isinstance(U, int) and U == units - 1)
                    if s == QUERY_TURN - 1 and more:
                        high_part(U + 1, 1 - u)
                    if s == 0 and V2 is not None:
                        take_back(V2, u, 1)
                    if V is not None:
                        behind(V, 1 - u, s)
                    W, same, i = lagged(U, V, s, LAG_TURN)
                    if W is not None:
                        take_turned(W, i)
                    W, same, i = lagged(U, V, s, LAG_EXP)
                    if W is not None:
                        exponent(W, u if same else 1 - u, i)
                    if s == 3 and more:
                        take_destinations(U + 1, 1 - u)

            high_part(0, 0)
            take_destinations(0, 0)

            def tail(V, V2):
                take_back(V2, 0, 1)
                for s in range(NT):
                    behind(V, 1, s)
                    if s == 0:
                        exponent(V, 1, NT - 1)
                    if s < LAG_TURN:
                        take_turned(V, s - LAG_TURN + NT)
                take_back(V, 1, 1)
            run(act, unit, tail)

        @block.gpsimd
        def _(pool):
            def normalise(V, v, i):
                wait_apart(pool, inv_in, V * NT + i + 1, pool_passed)
                pool.tensor_scalar(e[:, i % 4, :], e[:, i % 4, :], row_inv[:, v, i:i + 1], 1.0,
                                   ALU.mult, ALU.mult).then_inc(normed, 1)

            def low_part(W, w):
                if kind != HEAD_UNITS:
                    return
                wait_apart(pool, q_whole_in, W + 1, pool_passed)
                half = slice(HALF, N)
                pool.tensor_tensor(q_low[w][:, half], q_whole[:, :], q_high[w][:, half].bitcast(F32),
                                   ALU.subtract).then_inc(q_low_in, 1)

            def copy(out, source):
                return pool.tensor_copy(out, source)

            def of_head(tensor, U):
                return tensor[:, U % HEADS]

            def copy_gram(W, w):
                if kind == HEAD_UNITS:
                    wait_apart(pool, q_mm, W - 1, pool_passed)
                    copy(gram[w][:, :, :], of_head(head_gram, W)).then_inc(gram_in, 1)

            def copy_head(W, w):
                if kind == HEAD_UNITS:
                    wait_apart(pool, out_mm, W - 1, pool_passed)
                    copy(w_now[w][:, :], of_head(head_w, W))
                    copy(ow_now[w][:, :], of_head(out_w, W))
                    copy(b_now[w][:, :], of_head(head_b, W)).then_inc(back_in, 1)

            def leaky(V, half):
                if kind == HEAD_UNITS:
                    pool.wait_ge(biased, 2 * V + half + 1)
                    pool.tensor_tensor(cat[half][:, :], above[half][:, :], below[half][:, :],
                                       ALU.subtract).then_inc(cat_in, 1)

            def unit(U, u, V, V2):
                for s in range(NT):
                    if s == QUERY_TURN and not (isinstance(U, int) and U == units - 1):
                        low_part(U + 1, 1 - u)
                    if s == 1 and V2 is not None:
                        leaky(V2, 1)
                    if s == AFTER0 + 2 and V is not None:
                        leaky(V, 0)
                    W, same, i = lagged(U, V, s, LAG_RECIP)
                    if W is not None:
                        normalise(W, u if same else 1 - u, i)
                    if s == 0 and not (isinstance(U, int) and U == units - 1):
                        copy_gram(U + 1, 1 - u)
                    if s == 4:
                        copy_head(U, u)

            copy_gram(0, 0)
            low_part(0, 0)

            def tail(V, V2):
                for s in range(LAG_RECIP):
                    if s == 1:
                        leaky(V2, 1)
                    normalise(V, 1, s - LAG_RECIP + NT)
                leaky(V, 0)
                leaky(V, 1)
            run(pool, unit, tail)

        @block.sync
        def _(sync):
            def load(W, w):
                wait_count(sync, mixed_mm, 2 * (W - 1))
                sync.dma_start(val[w][:, :, :], values(batch(W))).then_inc(val_in[w], 16)
            load(0, 0)
            load(1, 1)
            with sync.Fori(2, units - 1, 2) as W:
                load(W, 0)
                load(W + 1, 1)


def layer_norm(nc, name, x_cur, res, finish, stores=(), clears=(), weights=(), beside=None):
    GROUPS = 4
    ROWS = NT * B // GROUPS
    ON_POOL = 2
    kind = finish[0]
    with ExitStack() as local:
        def sb(n, shape, dt=F32):
            return local.enter_context(nc.sbuf_tensor(f"{name}_{n}", shape, dt))

        def sem(n):
            return local.enter_context(nc.semaphore(f"{name}_{n}"))

        tmp = sb("tmp", [P, GROUPS, ROWS, C])
        total = sb("total", [P, GROUPS, ROWS])
        var = sb("var", [P, GROUPS, ROWS])
        std = sb("std", [P, GROUPS, ROWS])
        step, added, squared, rooted = sem("step"), sem("added"), sem("squared"), sem("rooted")
        if kind == "elu":
            negative_in, exp_in, scaled, stored = sem("negative_in"), sem("exp_in"), sem("scaled"), sem("stored")
        if kind == "leaky":
            bias = sb("bias", [P, C])
            bias_in = sem("bias_in")
        if weights:
            cleared, weights_in = sem("cleared"), sem("weights_in")
        block = local.enter_context(nc.Block())
        rows = "p t b c -> p (t b) c"
        per = NT // GROUPS
        X = [x_cur[:, g * per:(g + 1) * per].rearrange(rows) for g in range(GROUPS)]
        R = [res[:, g * per:(g + 1) * per].rearrange(rows) for g in range(GROUPS)]
        done = {}
        if beside:
            beside(local, block)

        def wide(a):
            return a.unsqueeze(2).broadcast_to([P, ROWS, C])

        @block.vector
        def _(dve):
            def does(what, g, ins):
                done[what, g] = len(done) + 1
                ins.then_inc(step, 1)

            def after(what, g):
                dve.wait_ge(step, done[what, g])

            def add(g):
                if kind == "leaky":
                    after("leaky", g)
                    does("add", g, dve.tensor_tensor(X[g], X[g], R[g], ALU.add))
                elif kind == "elu":
                    dve.wait_ge(added, g + 1)
                    does("add", g, dve.scalar_tensor_tensor(out=X[g], in0=tmp[:, g], scalar=-1.0, in1=X[g],
                                                            op0=ALU.add, op1=ALU.add))
                elif g == 0:
                    does("add", g, dve.tensor_tensor(X[g], X[g], R[g], ALU.add))

            def sums(g):
                if ("add", g) in done:
                    after("add", g)
                else:
                    dve.wait_ge(added, g)
                does("sum", g, dve.tensor_reduce(total[:, g], X[g], AX.X, ALU.add))

            def centre(g):
                after("sum", g)
                does("centre", g, dve.scalar_tensor_tensor(out=X[g], in0=wide(total[:, g]), scalar=-1.0 / C,
                                                           in1=X[g], op0=ALU.mult, op1=ALU.add))

            def variance(g):
                dve.wait_ge(squared, g + 1)
                does("squares", g, dve.tensor_reduce(var[:, g], tmp[:, g], AX.X, ALU.add))
                after("squares", g)
                does("variance", g, dve.tensor_scalar(var[:, g], var[:, g], 1.0 / C, EPS, ALU.mult, ALU.add))

            def scale(g):
                dve.wait_ge(rooted, g + 1)
                does("inverse", g, dve.reciprocal(std[:, g], std[:, g]))
                if g >= ON_POOL:
                    after("inverse", g)
                    does("scale", g, dve.tensor_tensor(X[g], X[g], wide(std[:, g]), ALU.mult))

            if kind == "leaky":
                for g in range(GROUPS):
                    dve.wait_ge(added, g + 1)
                    does("leaky", g, dve.scalar_tensor_tensor(out=R[g], in0=R[g], scalar=LEAK_HEADS, in1=R[g],
                                                              op0=ALU.mult, op1=ALU.max))
            for g in range(GROUPS + 1):
                if g < GROUPS:
                    add(g)
                    sums(g)
                if g >= 1:
                    variance(g - 1)
                if g < GROUPS:
                    centre(g)
                if g >= 2:
                    scale(g - 2)
            scale(GROUPS - 1)

        @block.scalar
        def _(act):
            def exponent(g):
                act.activation(tmp[:, g], R[g], ACT.Relu, scale=-1.0).then_inc(negative_in, 1)
                act.wait_ge(negative_in, g + 1)
                act.activation(tmp[:, g], tmp[:, g], ACT.Exp, scale=-1.0)
                act.activation(R[g], R[g], ACT.Relu).then_inc(exp_in, 1)

            def square(g):
                act.wait_ge(step, done["centre", g])
                act.activation(tmp[:, g], X[g], ACT.Square).then_inc(squared, 1)

            def root(g):
                act.wait_ge(step, done["variance", g])
                act.activation(std[:, g], var[:, g], ACT.Sqrt).then_inc(rooted, 1)

            ahead = GROUPS - 1 if kind == "elu" else 0
            for g in range(ahead):
                exponent(g)
            for g in range(GROUPS):
                square(g)
                if kind == "elu" and g == 0:
                    exponent(GROUPS - 1)
                root(g)

        @block.gpsimd
        def _(pool):
            for place in clears:
                pool.memset(place, 0.0).then_inc(cleared, 1)
            if kind == "leaky":
                pool.wait_ge(bias_in, 16)
                for g in range(GROUPS):
                    pool.tensor_tensor(R[g], R[g], bias[:, :].unsqueeze(1).broadcast_to([P, ROWS, C]),
                                       ALU.add).then_inc(added, 1)
            else:
                for g in range(0 if kind == "elu" else 1, GROUPS):
                    if kind == "elu":
                        pool.wait_ge(exp_in, g + 1)
                    pool.tensor_tensor(X[g], X[g], R[g], ALU.add).then_inc(added, 1)
            for g in range(ON_POOL):
                pool.wait_ge(step, done["inverse", g])
                last = pool.tensor_tensor(X[g], X[g], wide(std[:, g]), ALU.mult)
                if kind == "elu":
                    last.then_inc(scaled, 1)

        @block.sync
        def _(sync):
            if kind == "leaky":
                sync.dma_start(bias[:, :], finish[1]).then_inc(bias_in, 16)
            if weights:
                sync.wait_ge(cleared, len(clears))
                for out, source in weights:
                    sync.dma_start(out, source).then_inc(weights_in, 16)
                sync.wait_ge(weights_in, 16 * len(weights))
            for t, (out, source) in enumerate(stores):
                g = t // per
                if g < ON_POOL:
                    sync.wait_ge(scaled, g + 1)
                else:
                    sync.wait_ge(step, done["scale", g])
                sync.dma_start(out, source).then_inc(stored, 16)
            if stores:
                sync.wait_ge(stored, 16 * len(stores))


def turn_graph(nc, local, block, k, graph_t):
    banks = [local.enter_context(nc.psum_tensor(f"pg{i}", [P, HALF], F32))[:, :] for i in range(4)]
    g_turned, g_in = local.enter_context(nc.semaphore("g_turned")), local.enter_context(nc.semaphore("g_in"))
    BLOCKS = NT * 2

    @block.tensor
    def _(pe):
        for n in range(BLOCKS):
            mt, half = n // 2, n % 2
            wait_count(pe, g_in, n - 3)
            for t in range(TPH):
                last = pe.transpose(banks[n % 4][:, at(0, t, P)], k["graph"][:, half * TPH + t, at(0, mt, P)],
                                    k["ident"][:, :])
            last.then_inc(g_turned, 1)

    @block.scalar
    def _(act):
        for n in range(BLOCKS):
            act.wait_ge(g_turned, n + 1)
            act.activation(graph_t[:, n // 2, at(0, n % 2, HALF)], banks[n % 4], ACT.Copy).then_inc(g_in, 1)


def chebyshev(nc, k, x_cur, res, graph_t, embedding, weight, bias):
    with ExitStack() as local:
        def sb(name, shape, dt=F32):
            return local.enter_context(nc.sbuf_tensor(name, shape, dt))

        def sem(name):
            return local.enter_context(nc.semaphore(name))

        t1 = sb("t1", [P, NT, B * C])
        t2 = sb("t2", [P, NT, B * C])
        emb = sb("emb", [P, NT, EMB])
        emb_t = sb("emb_t", [EMB, NT, P])
        bias_in = sb("bias_in", [EMB, C])
        bias_now = sb("bias_now", [P, NT, C])
        w_whole = sb("w_whole", [P, ORDERS, EMB * C])
        w_part = [sb(f"w_part{i}", [P, ORDERS, EMB * C], F32R) for i in range(2)]
        joined = [sb(f"joined{i}", [P, B, ORDERS, 2, C], F32R) for i in range(2)]
        joined_t = [sb(f"joined_t{i}", [P, ORDERS, P], F32R) for i in range(2)]
        prods = w_whole[:, 0:2, :].rearrange("p a (d c) -> p a d c", c=C)
        banks = [local.enter_context(nc.psum_tensor(f"pc{i}", [P, HALF], F32))[:, :] for i in range(4)]
        y = local.enter_context(nc.psum_tensor("cheb_y", [P, 2, EMB * C], F32))
        w_in, w_high, w_low = sem("w_inc"), sem("w_high"), sem("w_low")
        t_mm, t_in, e_mm, e_in = sem("t_mm"), sem("t_in"), sem("e_mmc"), sem("e_inc")
        high_in, join_in, join_mm, join_t_in = sem("high_inc"), sem("join_in"), sem("join_mm"), sem("join_t_in")
        y_mm, prod_in, sum_in = sem("y_mm"), sem("prod_inc"), sem("sum_in")
        pool_passed = sem("pool_passedc")
        block = local.enter_context(nc.Block())
        SOURCES = (x_cur.rearrange("p t b c -> p t (b c)"), t1, t2)

        @block.sync
        def _(sync):
            sync.dma_start(emb[:, :, :], embedding.rearrange("(t p) d -> p t d", p=P)).then_inc(w_in, 16)
            sync.dma_start(bias_in[:, :], bias).then_inc(w_in, 16)
            for order in range(ORDERS):
                for q in (0, C):
                    sync.dma_start(w_whole[q:q + C, order, :].rearrange("p (d o) -> p d o", d=EMB),
                                   weight[:, order].rearrange("d i o -> i d o")).then_inc(w_in, 16)

        @block.tensor
        def _(pe):
            for order in range(2):
                for t in range(NT):
                    n = order * NT + t
                    wait_count(pe, t_in, n - 3 if t or not order else n)
                    for m in range(NT):
                        last = pe.matmul(banks[n % 4], graph_t[:, m, at(0, t, P)], SOURCES[order][:, m, :],
                                         start=m == 0, stop=m == NT - 1)
                    last.then_inc(t_mm, 1)
            pe.wait_ge(w_in, 128)
            for t in range(NT):
                last = pe.transpose(y[0:EMB, 0, at(0, t, P)], emb[:, t, :], k["ident"][:, :])
            last.then_inc(e_mm, 1)
            pe.wait_ge(e_in, 1)
            for t in range(NT):
                last = pe.matmul(y[:, 1, at(0, t, C)], emb_t[:, t, :], bias_in[:, :], start=True, stop=True)
            last.then_inc(e_mm, 1)
            pe.wait_ge(t_in, 2 * NT)

            def turn(t, half, b):
                n = t * B + b
                if b == 0:
                    pe.wait_ge(join_in, t + 1)
                wait_count(pe, join_t_in, n - 1)
                for order in range(ORDERS):
                    last = pe.transpose(banks[b % 2][:, at(0, order, P)],
                                        joined[half][:, b, order].rearrange("p a c -> p (a c)").bitcast(F32),
                                        k["ident"][:, :])
                last.then_inc(join_mm, 1)

            def products(t, b):
                n = t * B + b
                pe.wait_ge(join_t_in, n + 1)
                wait_count(pe, prod_in, n - 1)
                for order in range(ORDERS):
                    for part in range(2):
                        for h in range(2):
                            last = pe.matmul(y[:, b % 2, at(0, h, HALF)], joined_t[b % 2][:, order, :],
                                             w_part[part][:, order, at(0, h, HALF)],
                                             start=order + part == 0, stop=order == ORDERS - 1 and part == 1)
                last.then_inc(y_mm, 1)

            def tile(t, half, more=True):
                for b in range(B):
                    if b < B - 1:
                        turn(t, half, b + 1)
                    elif more:
                        turn(t + 1, 1 - half, 0)
                    products(t, b)
            turn(0, 0, 0)
            pe.wait_ge(w_low, 1)
            pe.wait_ge(e_in, 2)
            tile(0, 0)
            with pe.Fori(1, NT - 2, 2) as t:
                tile(t, 1)
                tile(t + 1, 0)
            tile(NT - 1, 1, more=False)

        @block.scalar
        def _(act):
            act.wait_ge(w_in, 128)
            act.activation(w_part[0][:, :, :], w_whole[:, :, :], ACT.Copy).then_inc(w_high, 1)
            act.wait_ge(e_mm, 1)
            act.activation(emb_t[:, :, :], y[0:EMB, 0, :].rearrange("p (t n) -> p t n", t=NT), ACT.Copy).then_inc(e_in, 1)
            act.wait_ge(e_mm, 2)
            act.activation(bias_now[:, :, :], y[:, 1, 0:NT * C].rearrange("p (t c) -> p t c", t=NT), ACT.Copy).then_inc(e_in, 1)

            def tile(t):
                for b in range(B):
                    n = t * B + b
                    act.wait_ge(join_mm, n + 1)
                    wait_count(act, y_mm, n - 1)
                    act.activation(joined_t[b % 2][:, :, :],
                                   banks[b % 2][:, 0:ORDERS * P].rearrange("p (j n) -> p j n", j=ORDERS),
                                   ACT.Copy).then_inc(join_t_in, 1)
            tile(0)
            with act.Fori(1, NT) as t:
                tile(t)

        @block.gpsimd
        def _(pool):
            pool.wait_ge(w_high, 1)
            pool.tensor_tensor(w_part[1][:, :, :], w_whole[:, :, :], w_part[0][:, :, :].bitcast(F32),
                               ALU.subtract).then_inc(w_low, 1)
            pool.wait_ge(t_in, 2 * NT)

            def join(t, half):
                wait_apart(pool, join_mm, (t - 1) * B, pool_passed)
                for order, source in enumerate(SOURCES):
                    pool.tensor_copy(joined[half][:, :, order, 0, :],
                                     source[:, t, :].rearrange("p (b c) -> p b c", b=B)).then_inc(high_in, 1)
                for order, source in enumerate(SOURCES):
                    wait_apart(pool, high_in, ORDERS * t + order + 1, pool_passed)
                    last = pool.tensor_tensor(joined[half][:, :, order, 1, :],
                                              source[:, t, :].rearrange("p (b c) -> p b c", b=B),
                                              joined[half][:, :, order, 0, :].bitcast(F32), ALU.subtract)
                last.then_inc(join_in, 1)

            def add_bias(t):
                wait_apart(pool, sum_in, (t + 1) * B, pool_passed)
                pool.tensor_tensor(res[:, t], res[:, t], bias_now[:, t, :].unsqueeze(1).broadcast_to([P, B, C]), ALU.add)
            join(0, 0)
            join(1, 1)
            pool.wait_ge(e_in, 2)
            with pool.Fori(2, NT - 1, 2) as t:
                join(t, 0)
                add_bias(t - 2)
                join(t + 1, 1)
                add_bias(t - 1)
            add_bias(NT - 2)
            add_bias(NT - 1)

        @block.vector
        def _(dve):
            for n in range(2 * NT):
                t = n % NT
                dve.wait_ge(t_mm, n + 1)
                if n < NT:
                    dve.tensor_copy(t1[:, t, :], banks[n % 4]).then_inc(t_in, 1)
                else:
                    dve.scalar_tensor_tensor(out=t2[:, t, :], in0=banks[n % 4], scalar=2.0,
                                             in1=x_cur[:, t].rearrange("p b c -> p (b c)"),
                                             op0=ALU.mult, op1=ALU.subtract).then_inc(t_in, 1)
            dve.wait_ge(w_in, 128)
            dve.wait_ge(w_low, 1)

            def product(t, b):
                n = t * B + b
                dve.wait_ge(y_mm, n + 1)
                wait_count(dve, sum_in, n - 1)
                dve.tensor_tensor(prods[:, b % 2], y[:, b % 2].rearrange("p (d c) -> p d c", c=C),
                                  emb[:, t, :].unsqueeze(2).broadcast_to([P, EMB, C]), ALU.mult).then_inc(prod_in, 1)

            def total(t, b):
                n = t * B + b
                dve.wait_ge(prod_in, n + 1)
                dve.tensor_reduce(res[:, t, b, :], prods[:, b % 2].rearrange("p d c -> p c d"), AX.X,
                                  ALU.add).then_inc(sum_in, 1)

            def tile(t, before):
                for b in range(B):
                    product(t, b)
                    if b:
                        total(t, b - 1)
                    elif before is not None:
                        total(before, B - 1)
            tile(0, None)
            with dve.Fori(1, NT) as t:
                tile(t, t - 1)
            total(NT - 1, B - 1)


def message_places(nc, ctx):
    return [ctx.enter_context(nc.sbuf_tensor(name, shape, F32))
            for name, shape in (("wn", [P, 3, P]), ("b1c", [P, 1]), ("b2c", [P, 1]), ("b2r", [P, C]))]


def message_weights(wn, b1c, b2c, b2r, W1, b1, W2, b2):
    weights = [(b2r[:, :], b2.unsqueeze(0).broadcast_to([P, C]))]
    for q in range(2):
        d = slice(q * C, (q + 1) * C)
        weights += [(wn[d, j, d], source) for j, source in enumerate((W1[:, 0:C], W1[:, C:2 * C], W2))]
        weights += [(b1c[d, :], b1.unsqueeze(1)), (b2c[d, :], b2.unsqueeze(1))]
    return {"clears": [wn[:, :, :]], "weights": weights}


def message_passing(nc, k, x_cur, res, graph_t, value, wn, b1c, b2c, b2r):
    with ExitStack() as local:
        def sb(name, shape, dt=F32):
            return local.enter_context(nc.sbuf_tensor(name, shape, dt))

        def sem(name):
            return local.enter_context(nc.semaphore(name))

        v = sb("v", [P, NT, B * C])
        v_t = sb("v_t", [P, PAIRS, N])
        effect = [sb(f"effect{i}", [P, HALF]) for i in range(2)]
        hidden = [sb(f"hidden{i}", [P, HALF]) for i in range(2)]
        wtr = sb("wtr", [P, 3, P])
        banks = [local.enter_context(nc.psum_tensor(f"pm{i}", [P, HALF], F32))[:, :] for i in range(8)]
        e_bank, h_bank, n_bank, t_bank = banks[0:2], banks[2:4], banks[4:6], banks[6:8]
        v_in, v_set = sem("v_in3"), sem("v_set")
        turned, taken = sem("turned3"), sem("taken3")
        e_mm, e_in, h_mm, h_in = sem("e_mm"), sem("e_in"), sem("h_mm3"), sem("h_in3")
        n_mm, n_in, t_mm, t_in = sem("n_mm"), sem("n_in"), sem("t_mm3"), sem("t_in3")
        block = local.enter_context(nc.Block())
        SETUP = 1 + 2 * PAIRS
        KINDS = 2 * PAIRS

        @block.sync
        def _(sync):
            sync.wait_ge(v_in, 1)
            sync.dma_start(v[0:1, 0, :].rearrange("p (b c) -> p b c", b=B),
                           value.unsqueeze(1).broadcast_to([1, B, C])).then_inc(v_set, 16)

        @block.tensor
        def _(pe):
            for j in range(3):
                last = pe.transpose(n_bank[0][:, at(0, j, P)], wn[:, j, :], k["ident"][:, :])
            last.then_inc(turned, 1)
            pe.wait_ge(v_set, 16)
            for g in range(2 * PAIRS):
                wait_count(pe, taken, g)
                for t in range(TPH):
                    last = pe.transpose(n_bank[(g + 1) % 2][:, at(0, t, P)],
                                        v[:, (g % 2) * TPH + t, at(0, g // 2, P)], k["ident"][:, :])
                last.then_inc(turned, 1)
            pe.wait_ge(taken, SETUP)

            def effects(r, g):
                pair, half = g // 2, g % 2
                n = r * KINDS + g
                if half == 0:
                    wait_count(pe, n_in, (r - 1) * KINDS + 2 * pair + 2)
                wait_count(pe, e_in, n - 1)
                for m in range(NT):
                    last = pe.matmul(e_bank[half], v[:, m, at(0, pair, P)], graph_t[:, m, at(0, half, HALF)],
                                     start=m == 0, stop=m == NT - 1)
                last.then_inc(e_mm, 1)

            def hiddens(r, g):
                pair, half = g // 2, g % 2
                n = r * KINDS + g
                wait_count(pe, t_in, (r - 1) * KINDS + g + 1)
                pe.wait_ge(e_in, n + 1)
                wait_count(pe, h_in, n - 1)
                pe.matmul(h_bank[half], wtr[:, 0, :], v_t[:, pair, at(0, half, HALF)], start=True, stop=False)
                pe.matmul(h_bank[half], wtr[:, 1, :], effect[half][:, :], start=False, stop=True).then_inc(h_mm, 1)

            def news(r, g):
                half = g % 2
                n = r * KINDS + g
                pe.wait_ge(h_in, n + 1)
                wait_count(pe, n_in, n - 1)
                for t in range(TPH):
                    last = pe.matmul(n_bank[half][:, at(0, t, P)], hidden[half][:, at(0, t, P)], wtr[:, 2, :],
                                     start=True, stop=True)
                last.then_inc(n_mm, 1)
                wait_count(pe, t_in, n - 1)
                pe.matmul(t_bank[half], wtr[:, 2, :], hidden[half][:, :], start=True, stop=True).then_inc(t_mm, 1)

            def step(r):
                for g in range(KINDS + 2):
                    if g < KINDS:
                        effects(r, g)
                    if 1 <= g <= KINDS:
                        hiddens(r, g - 1)
                    if g >= 2:
                        news(r, g - 2)
            step(0)
            with pe.Fori(1, STEPS) as r:
                step(r)

        @block.vector
        def _(dve):
            dve.tensor_copy(v[:, :, :], x_cur.rearrange("p t b c -> p t (b c)")).then_inc(v_in, 1)
            for g in range(SETUP):
                dve.wait_ge(turned, g + 1)
                if g == 0:
                    dve.tensor_copy(wtr[:, :, :], n_bank[0][:, 0:3 * P].rearrange("p (j n) -> p j n", j=3)).then_inc(taken, 1)
                else:
                    q = g - 1
                    dve.tensor_copy(v_t[:, q // 2, at(0, q % 2, HALF)], n_bank[g % 2]).then_inc(taken, 1)

            def step(r):
                for g in range(KINDS):
                    pair, half = g // 2, g % 2
                    n = r * KINDS + g
                    dve.wait_ge(n_mm, n + 1)
                    if half == 0:
                        dve.wait_ge(e_mm, n + 2)
                    dve.tensor_tensor(v[:, half * TPH:(half + 1) * TPH, at(0, pair, P)]
                                      .rearrange("p t (b c) -> p t b c", b=2),
                                      n_bank[half].rearrange("p (t b c) -> p t b c", t=TPH, b=2),
                                      b2r[:, :].unsqueeze(1).unsqueeze(1).broadcast_to([P, TPH, 2, C]),
                                      ALU.add).then_inc(n_in, 1)
            step(0)
            with dve.Fori(1, STEPS) as r:
                step(r)
            dve.wait_ge(n_in, STEPS * KINDS)
            dve.tensor_copy(res.rearrange("p t b c -> p t (b c)"), v[:, :, :])

        @block.scalar
        def _(act):
            def step(r):
                for g in range(KINDS + 2):
                    if g < KINDS:
                        half, n = g % 2, r * KINDS + g
                        act.wait_ge(e_mm, n + 1)
                        wait_count(act, h_mm, n - 1)
                        act.activation(effect[half][:, :], e_bank[half], ACT.Copy).then_inc(e_in, 1)
                    if 1 <= g <= KINDS:
                        half, n = (g - 1) % 2, r * KINDS + g - 1
                        act.wait_ge(h_mm, n + 1)
                        wait_count(act, t_mm, n - 1)
                        act.activation(hidden[half][:, :], h_bank[half], ACT.Relu, bias=b1c[:, 0:1]).then_inc(h_in, 1)
                    if g >= 2:
                        pair, half, n = (g - 2) // 2, g % 2, r * KINDS + g - 2
                        act.wait_ge(t_mm, n + 1)
                        act.activation(v_t[:, pair, at(0, half, HALF)], t_bank[half], ACT.Identity,
                                       bias=b2c[:, 0:1]).then_inc(t_in, 1)
            step(0)
            with act.Fori(1, STEPS) as r:
                step(r)


def graph_stack(nc, x, adj, L0_gnn_Wh, L0_gnn_bh, L0_gnn_W_out, L0_gnn_b_out, L1_gnn_embedding, L1_gnn_weight,
                L1_gnn_bias, L2_gnn_intervention_value, L2_gnn_W1, L2_gnn_b1, L2_gnn_W2, L2_gnn_b2, L3_gnn_W,
                L3_gnn_a, out):
    with ExitStack() as ctx:
        k = constants(nc, ctx)
        res = ctx.enter_context(nc.sbuf_tensor("res", [P, NT, B, C], F32))[:, :, :, :]
        xv = x.rearrange("b (t p) c -> p t b c", p=P)

        sums = res.rearrange("p t b c -> p t (b c)")
        with ExitStack() as layer:
            def sb(name, shape, dt=F32):
                return layer.enter_context(nc.sbuf_tensor(name, shape, dt))
            xs = sb("xs", [P, B, N], F32R)
            gram, head_w = sb("head_gram", [P, HEADS, 2, P], F32R), sb("head_w", [P, HEADS, HID])
            out_w, head_b = sb("out_w", [P, HEADS, C]), sb("head_b", [P, HEADS, 2])
            prepare_heads(nc, k, x, adj, L0_gnn_Wh, L0_gnn_bh, L0_gnn_W_out, xs, gram, head_w, out_w, head_b, sums)

            def x_of(b):
                if isinstance(b, int):
                    return x[b].rearrange("(t p) c -> p t c", p=P)
                return x[bass.ds(b, 1)].rearrange("a (t p) c -> p (a t) c", p=P)
            attention(nc, k, HEAD_UNITS, x_of, sums, xs, gram, head_w, out_w, head_b)

        def values_of(tensor):
            def of(b):
                if isinstance(b, int):
                    return tensor[:, :, b, :]
                return tensor[:, :, bass.ds(b, 1), :].rearrange("p t a c -> p t (a c)")
            return of

        x_cur_t = ctx.enter_context(nc.sbuf_tensor("x_cur", [P, NT, B, C], F32))
        x_cur = x_cur_t[:, :, :, :]

        with ExitStack() as layer:
            xs = layer.enter_context(nc.sbuf_tensor("xs2", [P, B, N], F32R))
            nat = layer.enter_context(nc.sbuf_tensor("nat2", [P, NT, B, C], F32))
            prepare_output_head(nc, k, sums, xs, nat, [(x_cur[:, t], xv[:, t]) for t in range(NT)])
            attention(nc, k, OUTPUT_UNITS, values_of(nat), res, xs)

        with ExitStack() as layer:
            graph_t = layer.enter_context(nc.sbuf_tensor("graph_t", [P, NT, N], F32))
            layer_norm(nc, "norm1", x_cur, res, ("leaky", L0_gnn_b_out.unsqueeze(0).broadcast_to([P, C])),
                       beside=lambda local, block: turn_graph(nc, local, block, k, graph_t))
            chebyshev(nc, k, x_cur, res, graph_t, L1_gnn_embedding, L1_gnn_weight, L1_gnn_bias)
            places = message_places(nc, layer)
            layer_norm(nc, "norm2", x_cur, res, ("none",),
                       **message_weights(*places, L2_gnn_W1, L2_gnn_b1, L2_gnn_W2, L2_gnn_b2))
            message_passing(nc, k, x_cur, res, graph_t, L2_gnn_intervention_value, *places)

        w2 = ctx.enter_context(nc.sbuf_tensor("w2", [P, P + 2], F32))
        a4 = ctx.enter_context(nc.sbuf_tensor("a4", [P, 4], F32))
        layer_norm(nc, "norm3", x_cur, res, ("none",), **edge_weights(w2, a4, L3_gnn_W, L3_gnn_a))

        with ExitStack() as layer:
            def sb(name, shape, dt=F32):
                return layer.enter_context(nc.sbuf_tensor(name, shape, dt))
            nat = sb("nat4", [P, NT, B, C])
            src_score, dst_w, x_pairs = sb("src_score", [P, B, NT]), sb("dst_w", [P, 2, P]), sb("x_pairs4", [P, PAIRS, N])
            prepare_edges(nc, k, x_cur.rearrange("p t b c -> p t (b c)"), w2, a4, nat, src_score, dst_w, x_pairs)
            attention(nc, k, EDGE_UNITS, values_of(nat), res, src_score=src_score, dst_w=dst_w, x_pairs=x_pairs)
        ov = out.rearrange("b (t p) c -> p t b c", p=P)
        layer_norm(nc, "norm4", x_cur, res, ("elu",), stores=[(ov[:, t], x_cur[:, t]) for t in range(NT)])


_INS = ['x', 'adj', 'L0_gnn_Wh', 'L0_gnn_bh', 'L0_gnn_W_out', 'L0_gnn_b_out', 'L1_gnn_embedding', 'L1_gnn_weight',
        'L1_gnn_bias', 'L2_gnn_intervention_value', 'L2_gnn_W1', 'L2_gnn_b1', 'L2_gnn_W2', 'L2_gnn_b2', 'L3_gnn_W',
        'L3_gnn_a']


def kernel(**inputs):
    import numpy as np
    import concourse.bacc as bacc
    from concourse import mybir as _mybir
    from concourse.bass_utils import run_bass_kernel_spmd

    nc = bacc.Bacc("TRN2", target_bir_lowering=False, num_devices=1)
    arrays, args = {}, []
    for name in _INS:
        a = np.ascontiguousarray(inputs[name])
        arrays[f"in_{name}"] = a
        args.append(nc.dram_tensor(f"in_{name}", a.shape, _mybir.dt.from_np(a.dtype), kind="ExternalInput").ap())
    out = nc.dram_tensor("out_0", (B, N, C), F32, kind="ExternalOutput").ap()
    graph_stack(nc, *args, out)
    r = run_bass_kernel_spmd(nc, [arrays], core_ids=[0])
    return r.results[0]["out_0"]
```
